# Optimizing a Trainium2 kernel written in Bass

```python
import numpy as np
import jax
import jax.numpy as jnp

def _softmax(x, axis=-1):
    return jax.nn.softmax(x, axis=axis)

def _gelu(x):
    return jax.nn.gelu(x, approximate=True)

def _silu(x):
    return jax.nn.silu(x)

def _sigmoid(x):
    return jax.nn.sigmoid(x)

def _layernorm(x, axis=-1, eps=1e-05):
    m = jnp.mean(x, axis=axis, keepdims=True)
    v = jnp.var(x, axis=axis, keepdims=True)
    return (x - m) / jnp.sqrt(v + eps)

def _scatter_add(tgt, idx, src, axis=0):
    return tgt.at[idx].add(src)

def _segment_sum(src, seg, n):
    return jax.ops.segment_sum(src, seg, n)
kernel_name = 'mk_gnn_preln_d2_gnn_r64_e169e1'

def setup_inputs(seed: int=0):
    np.random.seed(seed)
    _w = jnp.asarray

    def _rec_inputs():
        import jax
        import jax.numpy as jnp
        _gk = jax.random.key(seed)
        x = 7.22e-05 + 1 * jax.random.normal(jax.random.fold_in(_gk, 1), (256, 512), jnp.float32)
        src = jax.random.randint(jax.random.fold_in(_gk, 2), (4096,), 0, 256, jnp.int32)
        dst = jnp.minimum((256 * jax.random.uniform(jax.random.fold_in(_gk, 3), (4096,)) ** 2.0).astype(jnp.int32), 16383)
        _o = jnp.argsort(dst, stable=True)
        src = src[_o]
        dst = dst[_o]
        return (x, src, dst)
    x, src, dst = _rec_inputs()

    def _L0_gnn_setup():
        import jax, jax.numpy as jnp
        import numpy as np
        N, E, H, L, G = (256, 2500, 512, 7, 128)
        LN_EPS = 1e-05
        EPS = 1e-07

        def _ln(x, g, b):
            m = jnp.mean(x, axis=-1, keepdims=True)
            v = jnp.var(x, axis=-1, keepdims=True)
            return (x - m) * jax.lax.rsqrt(v + LN_EPS) * g + b

        def _genconv(h, src, dst, W, b):
            msg = jax.nn.relu(h[src]) + EPS
            mmax = jax.ops.segment_max(msg, dst, num_segments=N)
            ex = jnp.exp(msg - mmax[dst])
            denom = jax.ops.segment_sum(ex, dst, num_segments=N)
            agg = jax.ops.segment_sum(msg * ex, dst, num_segments=N) / jnp.where(denom > 0, denom, 1.0)
            return (h + agg) @ W + b
        key = jax.random.key(seed)
        ks = jax.random.split(key, 8)
        s = 1.0 / np.sqrt(H)
        return {'x': jax.random.normal(ks[0], (N, H), jnp.float32), 'edge_index': jax.random.randint(ks[1], (2, E), 0, N), 'batch': jnp.sort(jax.random.randint(ks[2], (N,), 0, G)), 'gcn_W': jax.random.uniform(ks[3], (L, H, H), jnp.float32, -s, s), 'gcn_b': jnp.zeros((L, H), jnp.float32), 'norm_g': jnp.ones((L, H), jnp.float32), 'norm_b': jnp.zeros((L, H), jnp.float32), 'vn_emb': jnp.zeros((H,), jnp.float32), 'vn_W1': jax.random.uniform(ks[4], (L - 1, H, H), jnp.float32, -s, s), 'vn_b1': jnp.zeros((L - 1, H), jnp.float32), 'vn_g': jnp.ones((L - 1, H), jnp.float32), 'vn_beta': jnp.zeros((L - 1, H), jnp.float32), 'vn_W2': jax.random.uniform(ks[5], (L - 1, H, H), jnp.float32, -s, s), 'vn_b2': jnp.zeros((L - 1, H), jnp.float32)}
    _L0_gnn_all = _L0_gnn_setup()
    _L0_gnn_in = {k: v for k, v in _L0_gnn_all.items() if k in ('gcn_W', 'gcn_b', 'norm_g', 'norm_b', 'vn_emb', 'vn_W1', 'vn_b1', 'vn_g', 'vn_beta', 'vn_W2', 'vn_b2')}
    del _L0_gnn_all

    def _L1_gnn_setup():
        import jax, jax.numpy as jnp
        import numpy as np
        N_NODES = 100000
        N_EDGES = 12800
        D = 512
        L = 3
        LN_EPS = 1e-05
        key = jax.random.key(seed)
        ks = jax.random.split(key, 8)
        x = jax.random.normal(ks[0], (N_NODES, D), dtype=jnp.float32)
        edge_index = jax.random.randint(ks[1], (2, N_EDGES), 0, N_NODES, dtype=jnp.int32)
        scale = 1.0 / np.sqrt(D)
        W_l = jax.random.normal(ks[2], (L, D, D), dtype=jnp.float32) * scale
        W_r = jax.random.normal(ks[3], (L, D, D), dtype=jnp.float32) * scale
        b = jax.random.normal(ks[4], (L, D), dtype=jnp.float32) * 0.01
        ln_g = jnp.ones((L, D), dtype=jnp.float32)
        ln_b = jnp.zeros((L, D), dtype=jnp.float32)
        return {'x': x, 'edge_index': edge_index, 'W_l': W_l, 'W_r': W_r, 'b': b, 'ln_g': ln_g, 'ln_b': ln_b}
    _L1_gnn_all = _L1_gnn_setup()
    _L1_gnn_in = {k: v for k, v in _L1_gnn_all.items() if k in ('W_l', 'W_r', 'b', 'ln_g', 'ln_b')}
    del _L1_gnn_all
    return {'x': x, 'src': src, 'dst': dst, 'L0_gnn_gcn_W': _L0_gnn_in['gcn_W'], 'L0_gnn_gcn_b': _L0_gnn_in['gcn_b'], 'L0_gnn_norm_g': _L0_gnn_in['norm_g'], 'L0_gnn_norm_b': _L0_gnn_in['norm_b'], 'L0_gnn_vn_emb': _L0_gnn_in['vn_emb'], 'L0_gnn_vn_W1': _L0_gnn_in['vn_W1'], 'L0_gnn_vn_b1': _L0_gnn_in['vn_b1'], 'L0_gnn_vn_g': _L0_gnn_in['vn_g'], 'L0_gnn_vn_beta': _L0_gnn_in['vn_beta'], 'L0_gnn_vn_W2': _L0_gnn_in['vn_W2'], 'L0_gnn_vn_b2': _L0_gnn_in['vn_b2'], 'L1_gnn_W_l': _L1_gnn_in['W_l'], 'L1_gnn_W_r': _L1_gnn_in['W_r'], 'L1_gnn_b': _L1_gnn_in['b'], 'L1_gnn_ln_g': _L1_gnn_in['ln_g'], 'L1_gnn_ln_b': _L1_gnn_in['ln_b']}

def reference(x, src, dst, L0_gnn_gcn_W, L0_gnn_gcn_b, L0_gnn_norm_g, L0_gnn_norm_b, L0_gnn_vn_emb, L0_gnn_vn_W1, L0_gnn_vn_b1, L0_gnn_vn_g, L0_gnn_vn_beta, L0_gnn_vn_W2, L0_gnn_vn_b2, L1_gnn_W_l, L1_gnn_W_r, L1_gnn_b, L1_gnn_ln_g, L1_gnn_ln_b):
    import jax
    import jax.numpy as jnp

    def _L0_gnn_ref(x, edge_index, batch, gcn_W, gcn_b, norm_g, norm_b, vn_emb, vn_W1, vn_b1, vn_g, vn_beta, vn_W2, vn_b2):
        import jax, jax.numpy as jnp
        import numpy as np
        N, E, H, L, G = (256, 2500, 512, 7, 128)
        LN_EPS = 1e-05
        EPS = 1e-07

        def _ln(x, g, b):
            m = jnp.mean(x, axis=-1, keepdims=True)
            v = jnp.var(x, axis=-1, keepdims=True)
            return (x - m) * jax.lax.rsqrt(v + LN_EPS) * g + b

        def _genconv(h, src, dst, W, b):
            msg = jax.nn.relu(h[src]) + EPS
            mmax = jax.ops.segment_max(msg, dst, num_segments=N)
            ex = jnp.exp(msg - mmax[dst])
            denom = jax.ops.segment_sum(ex, dst, num_segments=N)
            agg = jax.ops.segment_sum(msg * ex, dst, num_segments=N) / jnp.where(denom > 0, denom, 1.0)
            return (h + agg) @ W + b
        src, dst = (edge_index[0], edge_index[1])
        vn = jnp.broadcast_to(vn_emb, (G, H))
        h = x + vn[batch]
        h = _genconv(h, src, dst, gcn_W[0], gcn_b[0])
        for l in range(1, L):
            h2 = jax.nn.relu(_ln(h, norm_g[l - 1], norm_b[l - 1]))
            vn_tmp = jax.ops.segment_sum(h2, batch, num_segments=G) + vn
            vn_hid = jax.nn.relu(_ln(vn_tmp @ vn_W1[l - 1] + vn_b1[l - 1], vn_g[l - 1], vn_beta[l - 1]))
            vn = vn_hid @ vn_W2[l - 1] + vn_b2[l - 1]
            h2 = h2 + vn[batch]
            h = _genconv(h2, src, dst, gcn_W[l], gcn_b[l]) + h
        h = _ln(h, norm_g[L - 1], norm_b[L - 1])
        return h

    def _L1_gnn_ref(x, edge_index, W_l, W_r, b, ln_g, ln_b):
        import jax, jax.numpy as jnp
        import numpy as np
        N_NODES = 100000
        N_EDGES = 12800
        D = 512
        L = 3
        LN_EPS = 1e-05
        src = edge_index[0]
        tgt = edge_index[1]
        n = x.shape[0]
        cnt = jax.ops.segment_sum(jnp.ones((src.shape[0],), x.dtype), tgt, num_segments=n)
        inv_cnt = (1.0 / jnp.maximum(cnt, 1.0))[:, None]
        for i in range(W_l.shape[0]):
            x_in = x
            agg = jax.ops.segment_sum(x[src], tgt, num_segments=n) * inv_cnt
            h = agg @ W_l[i].T + x @ W_r[i].T + b[i]
            mu = jnp.mean(h, axis=-1, keepdims=True)
            var = jnp.mean(jnp.square(h - mu), axis=-1, keepdims=True)
            h = (h - mu) * jax.lax.rsqrt(var + LN_EPS) * ln_g[i] + ln_b[i]
            h = jax.nn.relu(h)
            x = h + x_in
        return x
    edge_index = jnp.stack([src, dst])
    batch0 = jnp.zeros((256,), jnp.int32)
    h = jnp.maximum(_layernorm(x, axis=-1), 0.0)
    x = x + _L0_gnn_ref(h, edge_index, batch0, L0_gnn_gcn_W, L0_gnn_gcn_b, L0_gnn_norm_g, L0_gnn_norm_b, L0_gnn_vn_emb, L0_gnn_vn_W1, L0_gnn_vn_b1, L0_gnn_vn_g, L0_gnn_vn_beta, L0_gnn_vn_W2, L0_gnn_vn_b2)
    h = jnp.maximum(_layernorm(x, axis=-1), 0.0)
    x = x + _L1_gnn_ref(h, edge_index, L1_gnn_W_l, L1_gnn_W_r, L1_gnn_b, L1_gnn_ln_g, L1_gnn_ln_b)
    return x

_drawn_inputs = setup_inputs


def setup_inputs(seed=0):
    import zlib

    import numpy as np

    out = dict(_drawn_inputs(seed))
    spreads = {'L0_gnn_gcn_b': (0.0, 0.1),
     'L0_gnn_norm_g': (1.0, 0.2),
     'L0_gnn_norm_b': (0.0, 0.1),
     'L0_gnn_vn_emb': (0.0, 0.1),
     'L0_gnn_vn_b1': (0.0, 0.8),
     'L0_gnn_vn_g': (1.0, 0.2),
     'L0_gnn_vn_beta': (0.0, 0.276),
     'L0_gnn_vn_b2': (0.0, 0.1),
     'L1_gnn_ln_g': (1.0, 0.2),
     'L1_gnn_ln_b': (0.0, 0.1)}
    factors = {'L1_gnn_b': 8.0}
    for name, (base, spread) in spreads.items():
        noise = np.random.default_rng([zlib.crc32(name.encode()), seed]).standard_normal(out[name].shape)
        drawn = base * np.exp(spread * noise) if base else spread * noise
        out[name] = jnp.asarray(drawn.astype(out[name].dtype))
    for name, factor in factors.items():
        out[name] = (out[name] * factor).astype(out[name].dtype)
    return out
```

```python
import concourse.bass as bass
from concourse import mybir
from contextlib import ExitStack

F32 = mybir.dt.float32
F32R = mybir.dt.float32r
BF16 = mybir.dt.bfloat16
I32 = mybir.dt.int32
ALU = mybir.AluOpType
ACT = mybir.ActivationFunctionType
AX_X = mybir.AxisListType.X

P = 128
LN_EPS = 1e-5
MSG_EPS = 1e-7
EXP_SHIFT = 60.0
COLS = ("norm_g", "norm_b", "vn_b1", "vn_g", "vn_beta", "vn_b2")


class Steps:

    def __init__(self, eng, sem, per_loop):
        self.eng, self.sem, self.per_loop = eng, sem, per_loop
        self.base, self.n = 0, 0

    def enter(self, base):
        self.base, self.n = base, 0

    def leave(self):
        assert self.n == self.per_loop, self.n

    def did(self, ins):
        ins.then_inc(self.sem, 1)
        self.n += 1
        return self.base + self.n

    def wait(self, value):
        self.eng.wait_ge(self.sem, value)

    def then(self, ins):
        self.wait(self.did(ins))


def gnn_kernel(nc, x, src, dst, gcn_w, gcn_b, cols, last_g, last_b, vn_emb, vn_w1, vn_w2,
               sage_wl, sage_wr, sage_b, sage_g, sage_beta, out):
    N, H = x.shape
    E = src.shape[0]
    L = gcn_w.shape[0]
    M = sage_wl.shape[0]
    NT = N // P
    FC = H // P
    ET = E // P
    EU = 8
    NCOL = len(COLS)
    LAST = L - 1

    ctx = ExitStack()
    with ctx:
        def sb(name, shape, dt=F32):
            return ctx.enter_context(nc.sbuf_tensor(name, shape, dt))

        def pb(name, shape):
            return ctx.enter_context(nc.psum_tensor(name, shape, F32))

        def sem(name):
            return ctx.enter_context(nc.semaphore(name))

        ident = sb("ident", [P, P])
        iota = sb("iota", [P, N], BF16)
        ones = sb("ones", [P, P])
        ones_r = sb("ones_r", [P, P], F32R)
        mean_w = sb("mean_w", [P, P])
        neg_half = sb("neg_half", [P, NT])
        shift = sb("shift", [P, 1])
        edge_i = sb("edge_i", [P, 2, ET], I32)
        edge_f = sb("edge_f", [P, 2, ET])
        hot_src = sb("hot_src", [P, ET, N], BF16)
        hot_dst = sb("hot_dst", [P, ET, N], BF16)
        adj = sb("adj", [P, NT, N], F32R)
        has_in = sb("has_in", [P, N])
        no_in = sb("no_in", [P, N], F32R)
        inv_cnt = sb("inv_cnt", [P, N])
        cnt1 = sb("cnt1", [P, N])
        x0 = sb("x0", [P, NT, H])
        h = sb("h", [P, NT, H])
        hb = sb("hb", [P, NT, H])
        z = sb("z", [P, NT, H])
        ex = sb("ex", [P, NT, H])
        dex = sb("dex", [P, NT, H])
        ex_hi = sb("ex_hi", [P, NT, H], F32R)
        ex_lo = sb("ex_lo", [P, NT, H], F32R)
        dex_hi = sb("dex_hi", [P, NT, H], F32R)
        dex_lo = sb("dex_lo", [P, NT, H], F32R)
        xs = sb("xs", [P, NT, H])
        stats = sb("stats", [P, NT, 6])
        mv = sb("mv", [P, NT, 2])
        var_eps = sb("var_eps", [P, NT])
        rstd = sb("rstd", [P, NT])
        h2 = sb("h2", [P, FC, N])
        d = sb("d", [P, FC, N])
        c1 = sb("c1", [P, FC, N])
        c = sb("c", [P, FC, N])
        r = sb("r", [P, FC, N])
        q = sb("q", [P, FC, N])
        t = sb("t", [P, FC, N])
        h_sum = sb("h_sum", [P, FC])
        h_max = sb("h_max", [P, FC])
        vn = sb("vn", [P, FC])
        vsum = sb("vsum", [P, FC])
        v_pair = sb("v_pair", [P, FC, 2], F32R)
        u0 = sb("u0", [P, FC])
        u = sb("u", [P, FC])
        u_sum = sb("u_sum", [P, 1])
        uc = sb("uc", [P, FC])
        usq = sb("usq", [P, FC])
        usq_sum = sb("usq_sum", [P, 1])
        vvar = sb("vvar", [P, 1])
        vrstd = sb("vrstd", [P, 1])
        ug = sb("ug", [P, FC])
        ub = sb("ub", [P, FC])
        hid_pair = sb("hid_pair", [P, FC, 2], F32R)
        v0 = sb("v0", [P, FC])
        vne = sb("vne", [P, FC])
        gm0 = sb("gm0", [P, FC])
        gm = sb("gm", [P, FC])
        d_add = sb("d_add", [P, FC])
        d_min = sb("d_min", [P, FC])
        w = sb("w", [P, FC, H])
        bias = sb("bias", [P, H])
        col = sb("col", [P, NCOL, FC])
        w1 = sb("w1", [P, FC, H])
        w2 = sb("w2", [P, FC, H])
        w1_hi = sb("w1_hi", [P, FC, H], F32R)
        w1_lo = sb("w1_lo", [P, FC, H], F32R)
        w2_hi = sb("w2_hi", [P, FC, H], F32R)
        w2_lo = sb("w2_lo", [P, FC, H], F32R)
        wr = sb("wr", [P, FC, H])
        wl = sb("wl", [P, FC, H])
        s_bias = sb("s_bias", [1, H])
        s_g = sb("s_g", [P, H])
        s_beta = sb("s_beta", [P, H])
        fin_g = sb("fin_g", [P, H])
        fin_b = sb("fin_b", [P, H])

        ps_row = pb("ps_row", [P, NT, H])
        ps_zt = pb("ps_zt", [P, FC, N])
        ps_den = pb("ps_den", [P, FC, N])
        ps_num = pb("ps_num", [P, FC, N])
        ps_v1 = ps_num[:, 0, 0:2 * FC].rearrange("p (c e) -> p c e", e=2)
        ps_v2 = ps_num[:, 0, 2 * FC:4 * FC].rearrange("p (c e) -> p c e", e=2)
        ps_mean = ps_num[:, 2, 0:1]
        ps_var = ps_num[:, 2, 2:3]
        ps_adj = ps_den[:, 0:2, :]
        ps_cnt = ps_den[:, 2, :]

        x_in, edge_in, emb_in, w_in, w1_in, w2_in = (sem(s) for s in ("x_in", "edge_in", "emb_in", "w_in", "w1_in", "w2_in"))
        bias_in, col_in, fin_in = sem("bias_in"), sem("col_in"), sem("fin_in")
        wr_in, wl_in, srow_in, sgb_in = sem("wr_in"), sem("wl_in"), sem("srow_in"), sem("sgb_in")
        out_done = sem("out_done")
        const_ready, iota_ready, ones_ready, ident_ready = sem("const_ready"), sem("iota_ready"), sem("ones_ready"), sem("ident_ready")
        hot_ready, adj_done, adj_ready, cnt_done, graph_ready = (sem(s) for s in (
            "hot_ready", "adj_done", "adj_ready", "cnt_done", "graph_ready"))
        var_ready, rstd_ready, z_ready, h_ready = sem("var_ready"), sem("rstd_ready"), sem("z_ready"), sem("h_ready")
        zt_done = sem("zt_done")
        h2_ready = sem("h2_ready")
        vin_ready, vn1_done, usum_ready, mean_done, usq_ready, uvar_done, vvar_ready, vrstd_ready = (sem(s) for s in (
            "vin_ready", "vn1_done", "usum_ready", "mean_done", "usq_ready", "uvar_done", "vvar_ready", "vrstd_ready"))
        hid_ready, vn2_done, vn_ready = sem("hid_ready"), sem("vn2_done"), sem("vn_ready")
        w1_hi_ready, w1_lo_ready, w2_hi_ready, w2_lo_ready = (sem(s) for s in (
            "w1_hi_ready", "w1_lo_ready", "w2_hi_ready", "w2_lo_ready"))
        d_ready, dt_done = sem("d_ready"), sem("dt_done")
        ex_ready, ex_hi_ready, ex_lo_ready, dex_ready, dex_hi_ready, dex_lo_ready = (sem(s) for s in (
            "ex_ready", "ex_hi_ready", "ex_lo_ready", "dex_ready", "dex_hi_ready", "dex_lo_ready"))
        den_done, num_done, t_ready, row_done, hb_ready = (sem(s) for s in (
            "den_done", "num_done", "t_ready", "row_done", "hb_ready"))
        xs_ready, xs_hi_ready, xs_lo_ready, xt_done, xt_ready, nsum_done, agg_ready, xr_done, srow_done = (
            sem(s) for s in ("xs_ready", "xs_hi_ready", "xs_lo_ready", "xt_done", "xt_ready", "nsum_done",
                             "agg_ready", "xr_done", "srow_done"))
        dve_steps, stats_seen = sem("dve_steps"), sem("stats_seen")
        out_ready = sem("out_ready")

        x_rows = x.rearrange("(t p) f -> p t f", p=P)
        out_rows = out.rearrange("(t p) f -> p t f", p=P)

        def spread(row):
            return row.partition_broadcast(P)

        def kchunks(mat):
            return mat.rearrange("(c p) f -> p c f", p=P)

        block = ctx.enter_context(nc.Block())

        @block.sync
        def _(sp):
            sp.dma_start(edge_i[:, 0, :], src.rearrange("(p j) -> p j", p=P)).then_inc(edge_in, 16)
            sp.dma_start(edge_i[:, 1, :], dst.rearrange("(p j) -> p j", p=P)).then_inc(edge_in, 16)
            sp.dma_start(x0[:], x_rows).then_inc(x_in, 16)
            sp.dma_start(vn[:], vn_emb).then_inc(emb_in, 16)
            sp.dma_start(w[:], kchunks(gcn_w[0])).then_inc(w_in, 16)
            sp.dma_start(bias[:], spread(gcn_b[0])).then_inc(bias_in, 16)
            sp.dma_start(col[:], cols[0]).then_inc(col_in, 16)
            sp.dma_start(w1[:], kchunks(vn_w1[0])).then_inc(w1_in, 16)
            sp.dma_start(w2[:], kchunks(vn_w2[0])).then_inc(w2_in, 16)

            def layer_inputs(l, first):
                if not first:
                    sp.wait_ge(w1_hi_ready, l - 1)
                    sp.wait_ge(w1_lo_ready, l - 1)
                    sp.dma_start(w1[:], kchunks(vn_w1[l - 1])).then_inc(w1_in, 16)
                    sp.wait_ge(w2_hi_ready, l - 1)
                    sp.wait_ge(w2_lo_ready, l - 1)
                    sp.dma_start(w2[:], kchunks(vn_w2[l - 1])).then_inc(w2_in, 16)
                    sp.wait_ge(vn_ready, l - 1)
                    sp.dma_start(col[:], cols[l - 1]).then_inc(col_in, 16)
                    sp.wait_ge(hb_ready, l - 1)
                else:
                    sp.wait_ge(h_ready, NT)
                sp.dma_start(bias[:], spread(gcn_b[l])).then_inc(bias_in, 16)
                sp.wait_ge(row_done, NT * l)
                sp.dma_start(w[:], kchunks(gcn_w[l])).then_inc(w_in, 16)

            layer_inputs(1, True)
            with sp.Fori(2, L) as l:
                layer_inputs(l, False)

            sp.dma_start(fin_g[:], spread(last_g)).then_inc(fin_in, 16)
            sp.dma_start(fin_b[:], spread(last_b)).then_inc(fin_in, 16)

            def sage_inputs(m):
                sp.dma_start(wr[:], kchunks(sage_wr[m])).then_inc(wr_in, 16)
                if not isinstance(m, int):
                    sp.wait_ge(srow_done, NT * m)
                sp.dma_start(s_bias[:], sage_b[bass.ds(m, 1), :]).then_inc(srow_in, 16)
                sp.dma_start(wl[:], kchunks(sage_wl[m])).then_inc(wl_in, 16)
                if not isinstance(m, int):
                    sp.wait_ge(xs_ready, NT * (m + 1))
                sp.dma_start(s_g[:], spread(sage_g[m])).then_inc(sgb_in, 16)
                sp.dma_start(s_beta[:], spread(sage_beta[m])).then_inc(sgb_in, 16)

            sage_inputs(0)
            with sp.Fori(1, M) as m:
                sp.wait_ge(xr_done, m)
                sage_inputs(m)
            sp.wait_ge(out_ready, 1)
            sp.dma_start(out_rows, h[:]).then_inc(out_done, 16)
            sp.wait_ge(out_done, 16)

        @block.gpsimd
        def _(pool):
            nc.gpsimd.iota(iota[:], pattern=[[1, N]], base=0, channel_multiplier=0,
                           allow_small_or_imprecise_dtypes=True).then_inc(iota_ready, 1)
            nc.gpsimd.memset(neg_half[:], -0.5).then_inc(const_ready, 1)
            nc.gpsimd.memset(ident[:], 0.0).then_inc(const_ready, 1)
            pool.wait_ge(const_ready, 2)
            nc.gpsimd.affine_select(out=ident[:], in_=ident[:], compare_op=ALU.not_equal, fill=1.0, base=0,
                                    pattern=[[-1, P]], channel_multiplier=1).then_inc(ident_ready, 1)
            nc.gpsimd.memset(ones[:], 1.0).then_inc(ones_ready, 1)
            nc.gpsimd.memset(mean_w[:], 1.0 / H).then_inc(ones_ready, 1)
            nc.gpsimd.memset(shift[:], EXP_SHIFT).then_inc(ones_ready, 1)

            def row_rstd(i):
                for n in range(NT):
                    pool.wait_ge(var_ready, NT * i + n + 1)
                    nc.gpsimd.tensor_tensor(rstd[:, n:n + 1], var_eps[:, n:n + 1], neg_half[:, n:n + 1],
                                            ALU.pow).then_inc(rstd_ready, 1)

            def low_half(l, full, hi, lo, full_in, hi_ready, used, lo_ready):
                pool.wait_ge(full_in, 16 * (l + 1))
                pool.wait_ge(hi_ready, l + 1)
                if used is not None:
                    pool.wait_ge(used, l)
                nc.gpsimd.tensor_tensor(lo[:], full[:], hi[:].bitcast(F32), ALU.subtract).then_inc(lo_ready, 1)

            def layer(l, net, more):
                if net:
                    pool.wait_ge(vvar_ready, l)
                    nc.gpsimd.tensor_tensor(vrstd[:], vvar[:], neg_half[:, 0:1], ALU.pow).then_inc(vrstd_ready, 1)
                if more:
                    low_half(l, w1, w1_hi, w1_lo, w1_in, w1_hi_ready, vn1_done if net else None, w1_lo_ready)
                if net:
                    pool.wait_ge(h_ready, NT * l)
                    pool.wait_ge(bias_in, 16 * (l + 1))
                    for n in range(NT):
                        ins = nc.gpsimd.tensor_tensor(hb[:, n, :], h[:, n, :], bias[:], ALU.add)
                    ins.then_inc(hb_ready, 1)
                if more:
                    low_half(l, w2, w2_hi, w2_lo, w2_in, w2_hi_ready, vn2_done if net else None, w2_lo_ready)
                row_rstd(l + 1)

            row_rstd(0)
            layer(0, False, True)
            with pool.Fori(1, LAST) as l:
                layer(l, True, True)
            layer(LAST, True, False)
            row_rstd(L + 1)
            with pool.Fori(0, M) as m:
                row_rstd(m + L + 2)

        @block.scalar
        def _(act):
            def high_half(l, full, hi, full_in, used, hi_ready):
                act.wait_ge(full_in, 16 * (l + 1))
                if used is not None:
                    act.wait_ge(used, l)
                nc.scalar.copy(hi[:], full[:]).then_inc(hi_ready, 1)

            def layer(l, net, more):
                if net:
                    act.wait_ge(col_in, 16 * l)
                for f in range(FC):
                    if f % 2 == 0:
                        act.wait_ge(zt_done, 2 * l + f // 2 + 1)
                    if net:
                        nc.scalar.activation(h2[:, f, :], ps_zt[:, f, :], ACT.Relu, bias=col[:, 1, f:f + 1],
                                             scale=col[:, 0, f:f + 1],
                                             accum_out=h_sum[:, f:f + 1]).then_inc(h2_ready, 1)
                    else:
                        nc.scalar.activation(h2[:, f, :], ps_zt[:, f, :], ACT.Relu).then_inc(h2_ready, 1)
                if more:
                    high_half(l, w1, w1_hi, w1_in, vn1_done if net else None, w1_hi_ready)
                if not net:
                    act.wait_ge(ones_ready, 3)
                for n in range(NT):
                    act.wait_ge(dt_done, NT * l + n + 1)
                    nc.scalar.activation(ex[:, n, :], ps_row[:, n, :], ACT.Exp, bias=shift[:]).then_inc(ex_ready, 1)
                for n in range(NT):
                    act.wait_ge(ex_ready, NT * l + n + 1)
                    nc.scalar.copy(ex_hi[:, n, :], ex[:, n, :]).then_inc(ex_hi_ready, 1)
                for n in range(NT):
                    act.wait_ge(dex_ready, NT * l + n + 1)
                    nc.scalar.copy(dex_hi[:, n, :], dex[:, n, :]).then_inc(dex_hi_ready, 1)
                if more:
                    high_half(l, w2, w2_hi, w2_in, vn2_done if net else None, w2_hi_ready)

            layer(0, False, True)
            with act.Fori(1, LAST) as l:
                layer(l, True, True)
            layer(LAST, True, False)

            with act.Fori(0, M) as m:
                for n in range(NT):
                    act.wait_ge(xs_ready, NT * m + n + 1)
                    nc.scalar.copy(ex_hi[:, n, :], xs[:, n, :]).then_inc(xs_hi_ready, 1)
                for f in range(0, FC, 2):
                    act.wait_ge(xt_done, 2 * m + f // 2 + 1)
                    nc.scalar.copy(h2[:, f:f + 2, :], ps_zt[:, f:f + 2, :]).then_inc(xt_ready, 1)

        @block.vector
        def _(dve):
            LAYER_STEPS = 31
            steps = Steps(dve, dve_steps, LAYER_STEPS)

            dve.wait_ge(ones_ready, 1)
            nc.vector.tensor_copy(ones_r[:], ones[:]).then_inc(const_ready, 1)
            dve.wait_ge(edge_in, 32)
            steps.then(nc.vector.tensor_copy(edge_f[:], edge_i[:]))
            dve.wait_ge(iota_ready, 1)
            with dve.Fori(0, ET // EU) as turn:
                for e in range(EU):
                    e = turn * EU + e
                    nc.vector.tensor_scalar(hot_src[:, e, :], iota[:], edge_f[:, 0, bass.ds(e, 1)], None,
                                            ALU.is_equal)
                    ins = nc.vector.tensor_scalar(hot_dst[:, e, :], iota[:], edge_f[:, 1, bass.ds(e, 1)], None,
                                                  ALU.is_equal)
                    ins.then_inc(hot_ready, 1)

            def row_stats(rows, n):
                got = steps.did(nc.vector.bn_stats(stats[:, n, :], rows))
                steps.wait(got)
                dve.sem_inc(stats_seen, 1)
                steps.then(nc.vector.bn_aggr(mv[:, n, :], stats[:, n, :]))
                nc.vector.tensor_scalar(var_eps[:, n:n + 1], mv[:, n, 1:2], LN_EPS, None, ALU.add).then_inc(var_ready, 1)

            def row_scaled(i, rows, n, to):
                dve.wait_ge(rstd_ready, NT * i + n + 1)
                return nc.vector.tensor_scalar(to, rows, mv[:, n, 0:1], rstd[:, n:n + 1], ALU.subtract, ALU.mult)

            dve.wait_ge(x_in, 16)
            for n in range(NT):
                row_stats(x0[:, n, :], n)
            for n in range(NT):
                row_scaled(0, x0[:, n, :], n, z[:, n, :]).then_inc(z_ready, 1)

            dve.wait_ge(adj_done, ET // EU)
            nc.vector.tensor_copy(adj[:], ps_adj).then_inc(adj_ready, 1)
            dve.wait_ge(cnt_done, 1)
            a = steps.did(nc.vector.tensor_scalar(has_in[:], ps_cnt, 1.0, None, ALU.min))
            b = steps.did(nc.vector.tensor_scalar(cnt1[:], ps_cnt, 1.0, None, ALU.max))
            steps.wait(a)
            nc.vector.tensor_scalar(no_in[:], has_in[:], -1.0, 1.0, ALU.mult, ALU.add).then_inc(graph_ready, 1)
            steps.wait(b)
            nc.vector.reciprocal(inv_cnt[:], cnt1[:]).then_inc(graph_ready, 1)

            def virtual_node(l):
                steps.then(nc.vector.tensor_tensor(vsum[:], h_sum[:], vn[:], ALU.add))
                steps.then(nc.vector.tensor_copy(v_pair[:, :, 0], vsum[:]))
                nc.vector.tensor_tensor(v_pair[:, :, 1], vsum[:], v_pair[:, :, 0].bitcast(F32),
                                        ALU.subtract).then_inc(vin_ready, 1)
                got_max = steps.did(nc.vector.tensor_reduce(h_max[:], h2[:], AX_X, ALU.max))
                dve.wait_ge(vn1_done, l)
                steps.then(nc.vector.tensor_reduce(u0[:], ps_v1, AX_X, ALU.add))
                nc.vector.scalar_tensor_tensor(out=u[:], in0=u0[:], scalar=0.0, in1=col[:, 2, :], op0=ALU.add,
                                               op1=ALU.add, accum_out=u_sum[:]).then_inc(usum_ready, 1)
                dve.wait_ge(mean_done, l)
                steps.then(nc.vector.tensor_scalar(uc[:], u[:], ps_mean, None, ALU.subtract))
                nc.vector.tensor_tensor_reduce(usq[:], uc[:], uc[:], 1.0, 0.0, ALU.mult, ALU.add,
                                               usq_sum[:]).then_inc(usq_ready, 1)
                dve.wait_ge(uvar_done, l)
                nc.vector.tensor_scalar(vvar[:], ps_var, LN_EPS, None, ALU.add).then_inc(vvar_ready, 1)
                dve.wait_ge(vrstd_ready, l)
                steps.then(nc.vector.scalar_tensor_tensor(out=ug[:], in0=uc[:], scalar=vrstd[:], in1=col[:, 3, :],
                                                          op0=ALU.mult, op1=ALU.mult))
                steps.then(nc.vector.tensor_tensor(ub[:], ug[:], col[:, 4, :], ALU.add))
                steps.then(nc.vector.tensor_scalar(hid_pair[:, :, 0], ub[:], 0.0, None, ALU.max))
                nc.vector.scalar_tensor_tensor(out=hid_pair[:, :, 1], in0=ub[:], scalar=0.0,
                                               in1=hid_pair[:, :, 0].bitcast(F32), op0=ALU.max,
                                               op1=ALU.subtract).then_inc(hid_ready, 1)
                dve.wait_ge(vn2_done, l)
                steps.then(nc.vector.tensor_reduce(v0[:], ps_v2, AX_X, ALU.add))
                nc.vector.tensor_tensor(vn[:], v0[:], col[:, 5, :], ALU.add).then_inc(vn_ready, 1)
                dve.wait_ge(vn_ready, l)
                return got_max

            def layer(l, net):
                dve.wait_ge(h2_ready, FC * (l + 1))
                if net:
                    got_max = virtual_node(l)
                else:
                    got_max = steps.did(nc.vector.tensor_reduce(h_max[:], h2[:], AX_X, ALU.max))
                    dve.wait_ge(emb_in, 16)
                steps.then(nc.vector.tensor_scalar(vne[:], vn[:], MSG_EPS, None, ALU.add))
                steps.wait(got_max)
                steps.then(nc.vector.tensor_tensor(gm0[:], h_max[:], vne[:], ALU.add))
                steps.then(nc.vector.tensor_scalar(gm[:], gm0[:], MSG_EPS, None, ALU.max))
                steps.did(nc.vector.tensor_tensor(d_add[:], vne[:], gm[:], ALU.subtract))
                steps.then(nc.vector.tensor_scalar(d_min[:], gm[:], -1.0, MSG_EPS, ALU.mult, ALU.add))
                for f in range(FC):
                    nc.vector.tensor_scalar(d[:, f, :], h2[:, f, :], d_add[:, f:f + 1], d_min[:, f:f + 1],
                                            ALU.add, ALU.max).then_inc(d_ready, 1)
                for f in range(FC):
                    made = steps.did(nc.vector.tensor_scalar(c1[:, f, :], has_in[:], gm[:, f:f + 1], vn[:, f:f + 1],
                                                             ALU.mult, ALU.add))
                steps.wait(made)
                got_c = steps.did(nc.vector.tensor_tensor(c[:], c1[:], h2[:], ALU.add))
                for n in range(NT):
                    dve.wait_ge(ex_ready, NT * l + n + 1)
                    nc.vector.tensor_tensor(dex[:, n, :], ps_row[:, n, :], ex[:, n, :], ALU.mult).then_inc(dex_ready, 1)
                for n in range(NT):
                    dve.wait_ge(ex_hi_ready, NT * l + n + 1)
                    nc.vector.tensor_tensor(ex_lo[:, n, :], ex[:, n, :], ex_hi[:, n, :].bitcast(F32),
                                            ALU.subtract).then_inc(ex_lo_ready, 1)
                for n in range(NT):
                    dve.wait_ge(dex_hi_ready, NT * l + n + 1)
                    nc.vector.tensor_tensor(dex_lo[:, n, :], dex[:, n, :], dex_hi[:, n, :].bitcast(F32),
                                            ALU.subtract).then_inc(dex_lo_ready, 1)
                steps.wait(got_c)

                def inverse(f):
                    dve.wait_ge(den_done, 2 * l + f // 2 + 1)
                    return steps.did(nc.vector.reciprocal(r[:, f, :], ps_den[:, f, :]))

                def quotient(f, inv):
                    dve.wait_ge(num_done, 2 * l + f // 2 + 1)
                    steps.wait(inv)
                    return steps.did(nc.vector.tensor_tensor(q[:, f, :], ps_num[:, f, :], r[:, f, :], ALU.mult))

                def total(f, quo):
                    steps.wait(quo)
                    nc.vector.tensor_tensor(t[:, f, :], q[:, f, :], c[:, f, :], ALU.add).then_inc(t_ready, 1)

                inv, quo = {0: inverse(0)}, {}
                for f in range(FC):
                    if f + 1 < FC:
                        inv[f + 1] = inverse(f + 1)
                    quo[f] = quotient(f, inv[f])
                    if f >= 1:
                        total(f - 1, quo[f - 1])
                total(FC - 1, quo[FC - 1])
                for n in range(NT):
                    dve.wait_ge(row_done, NT * l + n + 1)
                    if net:
                        dve.wait_ge(hb_ready, l)
                        add = hb[:, n, :]
                    else:
                        dve.wait_ge(bias_in, 16)
                        add = bias[:]
                    nc.vector.tensor_tensor(h[:, n, :], ps_row[:, n, :], add, ALU.add).then_inc(h_ready, 1)
                    dve.wait_ge(h_ready, NT * l + n + 1)
                    row_stats(h[:, n, :], n)
                for n in range(NT):
                    row_scaled(l + 1, h[:, n, :], n, z[:, n, :]).then_inc(z_ready, 1)

            layer(0, False)
            before = steps.n
            with dve.Fori(1, LAST) as l:
                steps.enter((l - 1) * LAYER_STEPS + before)
                layer(l, True)
                steps.leave()
            steps.enter(before + (LAST - 1) * LAYER_STEPS)
            layer(LAST, True)

            dve.wait_ge(fin_in, 32)
            dve.wait_ge(z_ready, NT * (L + 1))
            for n in range(NT):
                steps.then(nc.vector.tensor_tensor(z[:, n, :], z[:, n, :], fin_g[:], ALU.mult))
                steps.then(nc.vector.tensor_tensor(z[:, n, :], z[:, n, :], fin_b[:], ALU.add))
                steps.then(nc.vector.tensor_tensor(x0[:, n, :], x0[:, n, :], z[:, n, :], ALU.add))
                row_stats(x0[:, n, :], n)
            for n in range(NT):
                steps.then(row_scaled(L + 1, x0[:, n, :], n, z[:, n, :]))
                nc.vector.tensor_scalar(xs[:, n, :], z[:, n, :], 0.0, None, ALU.max).then_inc(xs_ready, 1)

            SAGE_STEPS = 10
            before = steps.base + steps.n
            sage_steps = Steps(dve, dve_steps, SAGE_STEPS)
            steps = sage_steps
            with dve.Fori(0, M) as m:
                steps.enter(m * SAGE_STEPS + before)
                for n in range(NT):
                    dve.wait_ge(xs_hi_ready, NT * m + n + 1)
                    nc.vector.tensor_tensor(ex_lo[:, n, :], xs[:, n, :], ex_hi[:, n, :].bitcast(F32),
                                            ALU.subtract).then_inc(xs_lo_ready, 1)
                dve.wait_ge(graph_ready, 2)
                for f in range(FC):
                    if f % 2 == 0:
                        dve.wait_ge(nsum_done, 2 * m + f // 2 + 1)
                    nc.vector.tensor_tensor(t[:, f, :], ps_num[:, f, :], inv_cnt[:], ALU.mult).then_inc(agg_ready, 1)
                for n in range(NT):
                    dve.wait_ge(srow_done, NT * m + n + 1)
                    row_stats(ps_row[:, n, :], n)
                dve.wait_ge(sgb_in, 32 * (m + 1))
                for n in range(NT):
                    steps.then(row_scaled(m + L + 2, ps_row[:, n, :], n, z[:, n, :]))
                    steps.then(nc.vector.tensor_tensor(z[:, n, :], z[:, n, :], s_g[:], ALU.mult))
                    steps.then(nc.vector.tensor_tensor(z[:, n, :], z[:, n, :], s_beta[:], ALU.add))
                    nc.vector.scalar_tensor_tensor(out=xs[:, n, :], in0=z[:, n, :], scalar=0.0, in1=xs[:, n, :],
                                                   op0=ALU.max, op1=ALU.add).then_inc(xs_ready, 1)
                steps.leave()
            dve.wait_ge(xs_ready, NT * (M + 1))
            nc.vector.tensor_tensor(h[:], x0[:], xs[:], ALU.add).then_inc(out_ready, 1)

        @block.tensor
        def _(pe):
            def count_edges(turn, first):
                for u in range(EU):
                    e = turn * EU + u
                    pe.wait_ge(hot_ready, e + 1)
                    for n in range(NT):
                        ins = nc.tensor.matmul(ps_adj[:, n, :], hot_src[:, e, n * P:(n + 1) * P],
                                               hot_dst[:, e, :], start=(first and u == 0 and n == 0),
                                               stop=True, skip_group_check=True)
                ins.then_inc(adj_done, 1)

            def transposed(i, rows, ready):
                for n in range(NT):
                    pe.wait_ge(ready, NT * i + n + 1)
                    for f in range(FC):
                        ins = nc.tensor.transpose(ps_zt[:, f, n * P:(n + 1) * P], rows[:, n, f * P:(f + 1) * P], ident[:])
                        if n == NT - 1 and f % 2 == 1:
                            ins.then_inc(zt_done if rows is z else xt_done, 1)

            def column_product(to, hi, lo, pair, done):
                for j in range(FC):
                    for k in range(FC):
                        for half in (hi, lo):
                            ins = nc.tensor.matmul(to[:, j, :], half[:, k, j * P:(j + 1) * P], pair[:, k, :],
                                                   start=(k == 0 and half is hi), stop=(k == FC - 1 and half is lo))
                ins.then_inc(done, 1)

            def virtual_node(l):
                pe.wait_ge(w1_hi_ready, l)
                pe.wait_ge(w1_lo_ready, l)
                pe.wait_ge(vin_ready, l)
                column_product(ps_v1, w1_hi, w1_lo, v_pair, vn1_done)
                pe.wait_ge(usum_ready, l)
                nc.tensor.matmul(ps_mean, mean_w[:], u_sum[:], start=True, stop=True).then_inc(mean_done, 1)
                pe.wait_ge(usq_ready, l)
                nc.tensor.matmul(ps_var, mean_w[:], usq_sum[:], start=True, stop=True).then_inc(uvar_done, 1)
                pe.wait_ge(w2_hi_ready, l)
                pe.wait_ge(w2_lo_ready, l)
                pe.wait_ge(hid_ready, l)
                column_product(ps_v2, w2_hi, w2_lo, hid_pair, vn2_done)

            def summed(to, n, halves, first, done):
                for f in range(FC):
                    for g, half in enumerate(halves):
                        ins = nc.tensor.matmul(to[:, f, :], half[:, n, f * P:(f + 1) * P], adj[:, n, :],
                                               start=(first and f % 2 == 0 and g == 0), stop=True,
                                               skip_group_check=True)
                    if n == NT - 1 and f % 2 == 1:
                        ins.then_inc(done, 1)

            def layer(l, net):
                transposed(l, z, z_ready)
                if net:
                    virtual_node(l)
                for n in range(NT):
                    for f in range(FC):
                        pe.wait_ge(d_ready, FC * l + f + 1)
                        ins = nc.tensor.transpose(ps_row[:, n, f * P:(f + 1) * P], d[:, f, n * P:(n + 1) * P], ident[:])
                    ins.then_inc(dt_done, 1)
                if not net:
                    pe.wait_ge(graph_ready, 1)
                for f in range(FC):
                    nc.tensor.matmul(ps_den[:, f, :], ones_r[0:1, :], no_in[0:1, :], start=(f % 2 == 0), stop=True,
                                     skip_group_check=True)
                for n in range(NT):
                    pe.wait_ge(ex_lo_ready, NT * l + n + 1)
                    summed(ps_den, n, (ex_hi, ex_lo), False, den_done)
                for n in range(NT):
                    pe.wait_ge(dex_lo_ready, NT * l + n + 1)
                    summed(ps_num, n, (dex_hi, dex_lo), n == 0, num_done)
                pe.wait_ge(w_in, 16 * (l + 1))
                for f in range(FC):
                    pe.wait_ge(t_ready, FC * l + f + 1)
                    for n in range(NT):
                        ins = nc.tensor.matmul(ps_row[:, n, :], t[:, f, n * P:(n + 1) * P], w[:, f, :],
                                               start=(f == 0), stop=(f == FC - 1))
                        if f == FC - 1:
                            ins.then_inc(row_done, 1)

            count_edges(0, True)
            with pe.Fori(1, ET // EU) as turn:
                count_edges(turn, False)
            pe.wait_ge(adj_ready, 1)
            pe.wait_ge(const_ready, 3)
            for n in range(NT):
                ins = nc.tensor.matmul(ps_cnt, ones_r[:], adj[:, n, :], start=(n == 0), stop=(n == NT - 1))
            ins.then_inc(cnt_done, 1)
            pe.wait_ge(ident_ready, 1)
            layer(0, False)
            with pe.Fori(1, L) as l:
                layer(l, True)

            with pe.Fori(0, M) as m:
                pe.wait_ge(srow_in, 16 * (m + 1))
                transposed(m, xs, xs_ready)
                for n in range(NT):
                    nc.tensor.matmul(ps_row[:, n, :], ones[0:1, :], s_bias[:], start=True, stop=False)
                for n in range(NT):
                    pe.wait_ge(xs_lo_ready, NT * m + n + 1)
                    summed(ps_num, n, (ex_hi, ex_lo), n == 0, nsum_done)
                pe.wait_ge(wr_in, 16 * (m + 1))
                for f in range(FC):
                    if f % 2 == 0:
                        pe.wait_ge(xt_ready, 2 * m + f // 2 + 1)
                    for n in range(NT):
                        ins = nc.tensor.matmul(ps_row[:, n, :], h2[:, f, n * P:(n + 1) * P], wr[:, f, :],
                                               start=False, stop=False)
                ins.then_inc(xr_done, 1)
                pe.wait_ge(wl_in, 16 * (m + 1))
                pe.wait_ge(agg_ready, FC * (m + 1))
                for n in range(NT):
                    for f in range(FC):
                        ins = nc.tensor.matmul(ps_row[:, n, :], t[:, f, n * P:(n + 1) * P], wl[:, f, :],
                                               start=False, stop=(f == FC - 1))
                    ins.then_inc(srow_done, 1)


_OUT = ((256, 512), "float32")


def kernel(**inputs):
    import numpy as np
    import concourse.bacc as bacc
    from concourse.bass_utils import run_bass_kernel_spmd

    def columns(v):
        v = np.asarray(v)
        return v.reshape(v.shape[0], -1, P).transpose(0, 2, 1)

    g = {k: np.asarray(v) for k, v in inputs.items()}
    nets = g["L0_gnn_vn_W1"].shape[0]
    arrays = {
        "x": g["x"], "src": g["src"], "dst": g["dst"],
        "gcn_w": g["L0_gnn_gcn_W"], "gcn_b": g["L0_gnn_gcn_b"],
        "cols": np.stack([columns(g["L0_gnn_" + k][:nets]) for k in COLS], axis=2),
        "last_g": g["L0_gnn_norm_g"][nets], "last_b": g["L0_gnn_norm_b"][nets],
        "vn_emb": columns(g["L0_gnn_vn_emb"][None])[0],
        "vn_w1": g["L0_gnn_vn_W1"], "vn_w2": g["L0_gnn_vn_W2"],
        "sage_wl": g["L1_gnn_W_l"].transpose(0, 2, 1), "sage_wr": g["L1_gnn_W_r"].transpose(0, 2, 1),
        "sage_b": g["L1_gnn_b"], "sage_g": g["L1_gnn_ln_g"], "sage_beta": g["L1_gnn_ln_b"],
    }
    arrays = {f"in_{k}": np.ascontiguousarray(v) for k, v in arrays.items()}
    nc = bacc.Bacc("TRN2", target_bir_lowering=False, num_devices=1)
    args = [nc.dram_tensor(k, v.shape, mybir.dt.from_np(v.dtype), kind="ExternalInput").ap() for k, v in arrays.items()]
    out = nc.dram_tensor("out_0", _OUT[0], mybir.dt.from_np(np.dtype(_OUT[1])), kind="ExternalOutput").ap()
    gnn_kernel(nc, *args, out)
    r = run_bass_kernel_spmd(nc, [arrays], core_ids=[0])
    return r.results[0]["out_0"]
```

```python
import concourse.bass as bass
from concourse import mybir
from contextlib import ExitStack

F32 = mybir.dt.float32
F32R = mybir.dt.float32r
BF16 = mybir.dt.bfloat16
I32 = mybir.dt.int32
ALU = mybir.AluOpType
ACT = mybir.ActivationFunctionType
AX_X = mybir.AxisListType.X

P = 128
LN_EPS = 1e-5
MSG_EPS = 1e-7
EXP_SHIFT = 32.0
WARM_NORM, WARM_RELU, WARM_HIDDEN, WARM_TOP, WARM_EXP = 8, 5, 6, 4, 6
COLS = ("norm_g", "norm_b", "vn_g", "vn_beta", "vn_b2")


class Steps:

    def __init__(self, eng, sem, per_loop):
        self.eng, self.sem, self.per_loop = eng, sem, per_loop
        self.base, self.n = 0, 0

    def enter(self, base):
        self.base, self.n = base, 0

    def leave(self):
        assert self.n == self.per_loop, self.n

    def did(self, ins):
        ins.then_inc(self.sem, 1)
        self.n += 1
        return self.base + self.n

    def wait(self, value):
        self.eng.wait_ge(self.sem, value)

    def then(self, ins):
        self.wait(self.did(ins))


def gnn_kernel(nc, x, src, dst, gcn_w, gcn_b, cols, last_g, last_b, vn_emb, vn_w1, vn_b1, vn_w2,
               sage_wl, sage_wr, sage_b, sage_g, sage_beta, out):
    N, H = x.shape
    E = src.shape[0]
    L = gcn_w.shape[0]
    M = sage_wl.shape[0]
    NT = N // P
    FC = H // P
    ET = E // P
    EU = 8
    NCOL = len(COLS)
    LAST = L - 1

    ctx = ExitStack()
    with ctx:
        def sb(name, shape, dt=F32):
            return ctx.enter_context(nc.sbuf_tensor(name, shape, dt))

        def pb(name, shape):
            return ctx.enter_context(nc.psum_tensor(name, shape, F32))

        def sem(name):
            return ctx.enter_context(nc.semaphore(name))

        ident = sb("ident", [P, P])
        iota = sb("iota", [P, N], BF16)
        ones = sb("ones", [P, P])
        ones_r = sb("ones_r", [P, P], F32R)
        neg_half = sb("neg_half", [P, NT])
        shift = sb("shift", [P, 1])
        edge_i = sb("edge_i", [P, 2, ET], I32)
        edge_f = sb("edge_f", [P, 2, ET])
        hot_src = sb("hot_src", [P, ET, N], BF16)
        hot_dst = sb("hot_dst", [P, ET, N], BF16)
        adj = sb("adj", [P, NT, N], F32R)
        has_in = sb("has_in", [P, N])
        no_in = sb("no_in", [P, N], F32R)
        inv_cnt = sb("inv_cnt", [P, N])
        cnt1 = sb("cnt1", [P, N])
        x0 = sb("x0", [P, NT, H])
        h = sb("h", [P, NT, H])
        hb = sb("hb", [P, NT, H])
        z = sb("z", [P, NT, H])
        ex = sb("ex", [P, NT, H])
        dex = sb("dex", [P, NT, H])
        ex_hi = sb("ex_hi", [P, NT, H], F32R)
        ex_lo = sb("ex_lo", [P, NT, H], F32R)
        dex_hi = sb("dex_hi", [P, NT, H], F32R)
        dex_lo = sb("dex_lo", [P, NT, H], F32R)
        xs = sb("xs", [P, NT, H])
        d = sb("d", [P, NT, H])
        top_row = sb("top_row", [1, H])
        floor_row = sb("floor_row", [P, H])
        stats = sb("stats", [P, NT, 6])
        mv = sb("mv", [P, NT, 2])
        var_eps = sb("var_eps", [P, NT])
        rstd = sb("rstd", [P, NT])
        h2 = sb("h2", [P, FC, N])
        e = sb("e", [P, FC, N])
        c = sb("c", [P, FC, N])
        r = sb("r", [P, FC, N])
        err = sb("err", [P, FC, N])
        pr = sb("pr", [P, FC, N])
        q = sb("q", [P, FC, N])
        lg = sb("lg", [P, FC, N])
        y = sb("y", [P, FC // 2, N])
        t = sb("t", [P, FC, N])
        h_sum = sb("h_sum", [P, FC])
        h_max = sb("h_max", [P, FC])
        neg_max = sb("neg_max", [P, FC])
        vn = sb("vn", [P, FC])
        vsum = sb("vsum", [P, FC])
        u = sb("u", [P, FC])
        picked = sb("picked", [P, FC, P])
        v_stats = sb("v_stats", [P, 2, 6])
        v_mv = sb("v_mv", [P, 2])
        vvar = sb("vvar", [P, 1])
        vrstd = sb("vrstd", [P, 1])
        ug = sb("ug", [P, FC])
        ub = sb("ub", [P, FC])
        hid = sb("hid", [P, FC])
        max_b2 = sb("max_b2", [P, FC])
        gm = sb("gm", [P, FC])
        w = sb("w", [P, FC, H])
        bias = sb("bias", [P, H])
        col = sb("col", [P, NCOL, FC])
        w1 = sb("w1", [P, FC, H])
        b1 = sb("b1", [1, H])
        w2 = sb("w2", [P, FC, H])
        wr = sb("wr", [P, FC, H])
        wl = sb("wl", [P, FC, H])
        s_bias = sb("s_bias", [1, H])
        s_g = sb("s_g", [P, H])
        s_beta = sb("s_beta", [P, H])
        fin_g = sb("fin_g", [P, H])
        fin_b = sb("fin_b", [P, H])

        ps_row = pb("ps_row", [P, NT, H])
        ps_zt = pb("ps_zt", [P, FC, N])
        ps_den = pb("ps_den", [P, FC, N])
        ps_num = pb("ps_num", [P, FC, N])
        ps_v = [ps_num[:, 0, :], ps_num[:, 2, :]]
        ps_top = [ps_zt[:, 0, :], ps_zt[:, 2, :]]
        ps_top_col = ps_num[:, 0, 0:FC]
        ps_adj = ps_den[:, 0:2, :]
        ps_cnt = ps_den[:, 2, :]

        x_in, edge_in, emb_in, w_in, w1_in, w2_in = (sem(s) for s in ("x_in", "edge_in", "emb_in", "w_in", "w1_in", "w2_in"))
        bias_in, col_in, fin_in = sem("bias_in"), sem("col_in"), sem("fin_in")
        wr_in, wl_in, srow_in, sgb_in = sem("wr_in"), sem("wl_in"), sem("srow_in"), sem("sgb_in")
        out_done = sem("out_done")
        const_ready, iota_ready, ones_ready, ident_ready = sem("const_ready"), sem("iota_ready"), sem("ones_ready"), sem("ident_ready")
        hot_ready, adj_done, adj_ready, cnt_done, graph_ready = (sem(s) for s in (
            "hot_ready", "adj_done", "adj_ready", "cnt_done", "graph_ready"))
        var_ready, rstd_ready, z_ready, h_ready = sem("var_ready"), sem("rstd_ready"), sem("z_ready"), sem("h_ready")
        zt_done = sem("zt_done")
        h2_ready = sem("h2_ready")
        vin_ready, vn1_done, vvar_ready, vrstd_ready = (sem(s) for s in (
            "vin_ready", "vn1_done", "vvar_ready", "vrstd_ready"))
        hid_ready, top_done, vn_ready = sem("hid_ready"), sem("top_done"), sem("vn_ready")
        max_ready, e_ready, et_done, d_ready = sem("max_ready"), sem("e_ready"), sem("et_done"), sem("d_ready")
        floor_ready, top_row_ready, top_col_done = (sem(s) for s in ("floor_ready", "top_row_ready", "top_col_done"))
        ex_ready, ex_hi_ready, ex_lo_ready, dex_ready, dex_hi_ready, dex_lo_ready = (sem(s) for s in (
            "ex_ready", "ex_hi_ready", "ex_lo_ready", "dex_ready", "dex_hi_ready", "dex_lo_ready"))
        den_done, num_done, t_ready, row_done, hb_ready = (sem(s) for s in (
            "den_done", "num_done", "t_ready", "row_done", "hb_ready"))
        xs_ready, xs_hi_ready, xs_lo_ready, xt_done, xt_ready, nsum_done, agg_ready, xr_done, srow_done = (
            sem(s) for s in ("xs_ready", "xs_hi_ready", "xs_lo_ready", "xt_done", "xt_ready", "nsum_done",
                             "agg_ready", "xr_done", "srow_done"))
        log_ready, inv_ready = sem("log_ready"), sem("inv_ready")
        dve_steps, stats_seen = sem("dve_steps"), sem("stats_seen")
        out_ready = sem("out_ready")

        x_rows = x.rearrange("(t p) f -> p t f", p=P)
        out_rows = out.rearrange("(t p) f -> p t f", p=P)

        def spread(row):
            return row.partition_broadcast(P)

        def kchunks(mat):
            return mat.rearrange("(c p) f -> p c f", p=P)

        block = ctx.enter_context(nc.Block())

        @block.sync
        def _(sp):
            sp.dma_start(edge_i[:, 0, :], src.rearrange("(p j) -> p j", p=P)).then_inc(edge_in, 16)
            sp.dma_start(edge_i[:, 1, :], dst.rearrange("(p j) -> p j", p=P)).then_inc(edge_in, 16)
            sp.dma_start(x0[:], x_rows).then_inc(x_in, 16)
            sp.dma_start(vn[:], vn_emb).then_inc(emb_in, 16)
            sp.dma_start(w[:], kchunks(gcn_w[0])).then_inc(w_in, 16)
            sp.dma_start(bias[:], spread(gcn_b[0])).then_inc(bias_in, 16)
            sp.dma_start(col[:], cols[0]).then_inc(col_in, 16)
            sp.dma_start(w1[:], kchunks(vn_w1[0])).then_inc(w1_in, 16)
            sp.dma_start(b1[:], vn_b1[0:1, :]).then_inc(w1_in, 16)
            sp.dma_start(w2[:], kchunks(vn_w2[0])).then_inc(w2_in, 16)

            def layer_inputs(l, first):
                if not first:
                    sp.wait_ge(vn1_done, 2 * (l - 1))
                    sp.dma_start(w1[:], kchunks(vn_w1[l - 1])).then_inc(w1_in, 16)
                    sp.dma_start(b1[:], vn_b1[bass.ds(l - 1, 1), :]).then_inc(w1_in, 16)
                    sp.wait_ge(top_done, 2 * l)
                    sp.dma_start(w2[:], kchunks(vn_w2[l - 1])).then_inc(w2_in, 16)
                    sp.wait_ge(vn_ready, l - 1)
                    sp.dma_start(col[:], cols[l - 1]).then_inc(col_in, 16)
                    sp.wait_ge(hb_ready, l - 1)
                else:
                    sp.wait_ge(row_done, NT)
                sp.dma_start(bias[:], spread(gcn_b[l])).then_inc(bias_in, 16)
                sp.wait_ge(row_done, NT * l)
                sp.dma_start(w[:], kchunks(gcn_w[l])).then_inc(w_in, 16)

            layer_inputs(1, True)
            with sp.Fori(2, L) as l:
                layer_inputs(l, False)

            sp.dma_start(fin_g[:], spread(last_g)).then_inc(fin_in, 16)
            sp.dma_start(fin_b[:], spread(last_b)).then_inc(fin_in, 16)

            def sage_inputs(m):
                sp.dma_start(wr[:], kchunks(sage_wr[m])).then_inc(wr_in, 16)
                if not isinstance(m, int):
                    sp.wait_ge(srow_done, NT * m)
                sp.dma_start(s_bias[:], sage_b[bass.ds(m, 1), :]).then_inc(srow_in, 16)
                sp.dma_start(wl[:], kchunks(sage_wl[m])).then_inc(wl_in, 16)
                if not isinstance(m, int):
                    sp.wait_ge(xs_ready, NT * (m + 1))
                sp.dma_start(s_g[:], spread(sage_g[m])).then_inc(sgb_in, 16)
                sp.dma_start(s_beta[:], spread(sage_beta[m])).then_inc(sgb_in, 16)

            sage_inputs(0)
            with sp.Fori(1, M) as m:
                sp.wait_ge(xr_done, m)
                sage_inputs(m)
            sp.wait_ge(out_ready, 1)
            sp.dma_start(out_rows, h[:]).then_inc(out_done, 16)
            sp.wait_ge(out_done, 16)

        @block.gpsimd
        def _(pool):
            nc.gpsimd.iota(iota[:], pattern=[[1, N]], base=0, channel_multiplier=0,
                           allow_small_or_imprecise_dtypes=True).then_inc(iota_ready, 1)
            nc.gpsimd.memset(neg_half[:], -0.5).then_inc(const_ready, 1)
            nc.gpsimd.memset(ident[:], 0.0).then_inc(const_ready, 1)
            pool.wait_ge(const_ready, 2)
            nc.gpsimd.affine_select(out=ident[:], in_=ident[:], compare_op=ALU.not_equal, fill=1.0, base=0,
                                    pattern=[[-1, P]], channel_multiplier=1).then_inc(ident_ready, 1)
            nc.gpsimd.memset(ones[:], 1.0).then_inc(ones_ready, 1)
            nc.gpsimd.memset(shift[:], EXP_SHIFT).then_inc(ones_ready, 1)

            def row_rstd(i):
                for n in range(NT):
                    pool.wait_ge(var_ready, NT * i + n + 1)
                    nc.gpsimd.tensor_tensor(rstd[:, n:n + 1], var_eps[:, n:n + 1], neg_half[:, n:n + 1],
                                            ALU.pow).then_inc(rstd_ready, 1)

            def layer(l, net):
                if net:
                    pool.wait_ge(vvar_ready, l)
                    nc.gpsimd.tensor_tensor(vrstd[:], vvar[:], neg_half[:, 0:1], ALU.pow).then_inc(vrstd_ready, 1)
                    pool.wait_ge(h_ready, NT * l)
                    pool.wait_ge(bias_in, 16 * (l + 1))
                    for n in range(NT):
                        ins = nc.gpsimd.tensor_tensor(hb[:, n, :], h[:, n, :], bias[:], ALU.add)
                    ins.then_inc(hb_ready, 1)
                row_rstd(l + 1)

            row_rstd(0)
            layer(0, False)
            with pool.Fori(1, L) as l:
                layer(l, True)
            row_rstd(L + 1)
            with pool.Fori(0, M) as m:
                row_rstd(m + L + 2)

        @block.scalar
        def _(act):
            nc.scalar.preload_act_table_set("natural_log_exp_and_others")

            def layer(l, net):
                if net:
                    act.wait_ge(col_in, 16 * l)
                    act.wait_ge(zt_done, 2 * l + 1)
                    for f in range(FC // 2):
                        nc.scalar.activation(h2[:, f, :], ps_zt[:, f, :], ACT.Relu, bias=col[:, 1, f:f + 1],
                                             scale=col[:, 0, f:f + 1],
                                             accum_out=h_sum[:, f:f + 1]).then_inc(h2_ready, 1)
                else:
                    for f in range(0, FC, 2):
                        act.wait_ge(zt_done, f // 2 + 1)
                        nc.scalar.activation(h2[:, f:f + 2, :], ps_zt[:, f:f + 2, :], ACT.Relu).then_inc(h2_ready, 1)
                    act.wait_ge(ones_ready, 2)
                act.wait_ge(max_ready, 2 * l + 1)
                for f in range(FC):
                    nc.scalar.activation(e[:, f, :], h2[:, f, :], ACT.Identity,
                                         bias=neg_max[:, f:f + 1]).then_inc(e_ready, 1)
                if net:
                    for g in range(2):
                        act.wait_ge(floor_ready, 2 * l + g + 1)
                        nc.scalar.copy(top_row[:, g * H // 2:(g + 1) * H // 2], ps_top[g][0:1, :]).then_inc(top_row_ready, 1)
                for n in range(NT):
                    act.wait_ge(d_ready, NT * l + n + 1)
                    nc.scalar.activation(ex[:, n, :], d[:, n, :], ACT.Exp, bias=shift[:]).then_inc(ex_ready, 1)
                    act.wait_ge(ex_ready, NT * l + n + 1)
                    nc.scalar.copy(ex_hi[:, n, :], ex[:, n, :]).then_inc(ex_hi_ready, 1)
                for n in range(NT):
                    act.wait_ge(dex_ready, NT * l + n + 1)
                    nc.scalar.copy(dex_hi[:, n, :], dex[:, n, :]).then_inc(dex_hi_ready, 1)
                for g in range(2):
                    act.wait_ge(den_done, 2 * l + g + 1)
                    nc.scalar.activation(lg[:, 2 * g:2 * g + 2, :], ps_den[:, 2 * g:2 * g + 2, :],
                                         ACT.Ln).then_inc(log_ready, 1)
                    act.wait_ge(log_ready, 2 * l + g + 1)
                    nc.scalar.activation(r[:, 2 * g:2 * g + 2, :], lg[:, 2 * g:2 * g + 2, :], ACT.Exp,
                                         scale=-1.0).then_inc(inv_ready, 1)
                for n in range(NT):
                    act.wait_ge(z_ready, NT * (l + 1) + n + 1)
                    nc.scalar.copy(h[:, n, :], ps_row[:, n, :]).then_inc(h_ready, 1)

            layer(0, False)
            with act.Fori(1, L) as l:
                layer(l, True)

            with act.Fori(0, M) as m:
                for n in range(NT):
                    act.wait_ge(xs_ready, NT * m + n + 1)
                    nc.scalar.copy(ex_hi[:, n, :], xs[:, n, :]).then_inc(xs_hi_ready, 1)
                for f in range(0, FC, 2):
                    act.wait_ge(xt_done, 2 * m + f // 2 + 1)
                    nc.scalar.copy(h2[:, f:f + 2, :], ps_zt[:, f:f + 2, :]).then_inc(xt_ready, 1)

        @block.vector
        def _(dve):
            LAYER_STEPS = 35
            steps = Steps(dve, dve_steps, LAYER_STEPS)

            dve.wait_ge(ones_ready, 1)
            nc.vector.tensor_copy(ones_r[:], ones[:]).then_inc(const_ready, 1)
            dve.wait_ge(edge_in, 32)
            steps.then(nc.vector.tensor_copy(edge_f[:], edge_i[:]))
            dve.wait_ge(iota_ready, 1)
            with dve.Fori(0, ET // EU) as turn:
                for e in range(EU):
                    e = turn * EU + e
                    nc.vector.tensor_scalar(hot_src[:, e, :], iota[:], edge_f[:, 0, bass.ds(e, 1)], None,
                                            ALU.is_equal)
                    ins = nc.vector.tensor_scalar(hot_dst[:, e, :], iota[:], edge_f[:, 1, bass.ds(e, 1)], None,
                                                  ALU.is_equal)
                    ins.then_inc(hot_ready, 1)

            def row_stats(rows, n):
                got = steps.did(nc.vector.bn_stats(stats[:, n, :], rows))
                steps.wait(got)
                dve.sem_inc(stats_seen, 1)
                steps.then(nc.vector.bn_aggr(mv[:, n, :], stats[:, n, :]))
                nc.vector.tensor_scalar(var_eps[:, n:n + 1], mv[:, n, 1:2], LN_EPS, None, ALU.add).then_inc(var_ready, 1)

            def row_scaled(i, rows, n, to):
                dve.wait_ge(rstd_ready, NT * i + n + 1)
                return nc.vector.tensor_scalar(to, rows, mv[:, n, 0:1], rstd[:, n:n + 1], ALU.subtract, ALU.mult)

            dve.wait_ge(x_in, 16)
            for n in range(NT):
                row_stats(x0[:, n, :], n)
            for n in range(NT):
                row_scaled(0, x0[:, n, :], n, z[:, n, :]).then_inc(z_ready, 1)

            dve.wait_ge(adj_done, ET // EU)
            nc.vector.tensor_copy(adj[:], ps_adj).then_inc(adj_ready, 1)
            dve.wait_ge(cnt_done, 1)
            a = steps.did(nc.vector.tensor_scalar(has_in[:], ps_cnt, 1.0, None, ALU.min))
            b = steps.did(nc.vector.tensor_scalar(cnt1[:], ps_cnt, 1.0, None, ALU.max))
            steps.wait(a)
            nc.vector.tensor_scalar(no_in[:], has_in[:], -1.0, 1.0, ALU.mult, ALU.add).then_inc(graph_ready, 1)
            steps.wait(b)
            nc.vector.reciprocal(inv_cnt[:], cnt1[:]).then_inc(graph_ready, 1)

            def largest(offset):
                steps.then(nc.vector.tensor_reduce(h_max[:], h2[:], AX_X, ALU.max))
                nc.vector.tensor_scalar(neg_max[:], h_max[:], -1.0, None, ALU.mult).then_inc(max_ready, 1)
                nc.vector.tensor_tensor(max_b2[:], h_max[:], offset, ALU.add).then_inc(max_ready, 1)

            def as_column(to, g):
                half = slice(g * FC // 2, (g + 1) * FC // 2)
                steps.then(nc.vector.tensor_tensor(picked[:, half, :], ps_v[g].rearrange("p (c q) -> p c q", q=P),
                                                   ident[:, None, :].broadcast_to([P, FC // 2, P]), ALU.mult))
                steps.then(nc.vector.tensor_reduce(to[:, half], picked[:, half, :], AX_X, ALU.add))

            def virtual_node(l):
                nc.vector.tensor_tensor(vsum[:], h_sum[:], vn[:], ALU.add).then_inc(vin_ready, 1)
                largest(col[:, 4, :])
                for g in range(2):
                    dve.wait_ge(vn1_done, 2 * l - 1 + g)
                    got_stats = steps.did(nc.vector.bn_stats(v_stats[:, g, :], ps_v[g]))
                    if g == 0:
                        as_column(u, 0)
                steps.wait(got_stats)
                dve.sem_inc(stats_seen, 1)
                steps.then(nc.vector.bn_aggr(v_mv[:], v_stats[:]))
                nc.vector.tensor_scalar(vvar[:], v_mv[:, 1:2], LN_EPS, None, ALU.add).then_inc(vvar_ready, 1)
                as_column(u, 1)
                steps.then(nc.vector.scalar_tensor_tensor(out=ug[:], in0=u[:], scalar=v_mv[:, 0:1], in1=col[:, 2, :],
                                                          op0=ALU.subtract, op1=ALU.mult))
                dve.wait_ge(vrstd_ready, l)
                steps.then(nc.vector.scalar_tensor_tensor(out=ub[:], in0=ug[:], scalar=vrstd[:], in1=col[:, 3, :],
                                                          op0=ALU.mult, op1=ALU.add))
                nc.vector.tensor_scalar(hid[:], ub[:], 0.0, None, ALU.max).then_inc(hid_ready, 1)

            def layer(l, net):
                if net:
                    dve.wait_ge(col_in, 16 * l)
                    dve.wait_ge(zt_done, 2 * l + 2)
                    for f in range(FC // 2, FC):
                        scaled = steps.did(nc.vector.tensor_scalar(
                            y[:, f - FC // 2, :], ps_zt[:, f, :], col[:, 0, f:f + 1], col[:, 1, f:f + 1],
                            ALU.mult, ALU.add))
                    steps.wait(scaled)
                    for f in range(FC // 2, FC):
                        made = steps.did(nc.vector.tensor_scalar(
                            h2[:, f, :], y[:, f - FC // 2, :], 0.0, 0.0, ALU.max, ALU.add,
                            accum_out=h_sum[:, f:f + 1]))
                    steps.wait(made)
                dve.wait_ge(h2_ready, 2 * (l + 1))
                if net:
                    virtual_node(l)
                else:
                    dve.wait_ge(emb_in, 16)
                    largest(vn[:])
                for g in range(2):
                    half = slice(g * H // 2, (g + 1) * H // 2)
                    dve.wait_ge(top_done, 2 * l + g + 1)
                    nc.vector.tensor_scalar(floor_row[:, half], ps_top[g], -1.0, 0.0,
                                            ALU.mult, ALU.min).then_inc(floor_ready, 1)
                    dve.wait_ge(floor_ready, 2 * l + g + 1)
                    if g == 0:
                        dve.wait_ge(et_done, NT * (l + 1))
                    for n in range(NT):
                        ins = nc.vector.tensor_tensor(d[:, n, half], ps_row[:, n, half], floor_row[:, half], ALU.max)
                        if g == 1:
                            ins.then_inc(d_ready, 1)
                for n in range(NT):
                    dve.wait_ge(ex_ready, NT * l + n + 1)
                    nc.vector.tensor_tensor(dex[:, n, :], d[:, n, :], ex[:, n, :], ALU.mult).then_inc(dex_ready, 1)
                    if n == 0:
                        if net:
                            dve.wait_ge(top_col_done, l)
                        got_gm = steps.did(nc.vector.tensor_scalar(gm[:], ps_top_col if net else max_b2[:], 0.0,
                                                                   MSG_EPS, ALU.max, ALU.add))
                        if net:
                            nc.vector.tensor_tensor(vn[:], ps_top_col, h_max[:], ALU.subtract).then_inc(vn_ready, 1)
                    dve.wait_ge(ex_hi_ready, NT * l + n + 1)
                    nc.vector.tensor_tensor(ex_lo[:, n, :], ex[:, n, :], ex_hi[:, n, :].bitcast(F32),
                                            ALU.subtract).then_inc(ex_lo_ready, 1)
                for n in range(NT):
                    dve.wait_ge(dex_hi_ready, NT * l + n + 1)
                    nc.vector.tensor_tensor(dex_lo[:, n, :], dex[:, n, :], dex_hi[:, n, :].bitcast(F32),
                                            ALU.subtract).then_inc(dex_lo_ready, 1)
                steps.wait(got_gm)
                for f in range(FC):
                    gathered = steps.did(nc.vector.scalar_tensor_tensor(
                        out=c[:, f, :], in0=has_in[:], scalar=gm[:, f:f + 1], in1=h2[:, f, :],
                        op0=ALU.mult, op1=ALU.add))
                steps.wait(gathered)
                if net:
                    dve.wait_ge(vn_ready, l)

                def error(f):
                    return steps.did(nc.vector.tensor_tensor(err[:, f, :], ps_den[:, f, :], r[:, f, :], ALU.mult))

                def product(f):
                    return steps.did(nc.vector.tensor_tensor(pr[:, f, :], ps_num[:, f, :], r[:, f, :], ALU.mult))

                def quotient(f, ready):
                    steps.wait(ready)
                    return steps.did(nc.vector.scalar_tensor_tensor(out=q[:, f, :], in0=err[:, f, :], scalar=-2.0,
                                                                    in1=pr[:, f, :], op0=ALU.add, op1=ALU.mult))

                def total(f, quo):
                    steps.wait(quo)
                    nc.vector.scalar_tensor_tensor(out=t[:, f, :], in0=c[:, f, :], scalar=vn[:, f:f + 1],
                                                   in1=q[:, f, :], op0=ALU.add, op1=ALU.subtract).then_inc(t_ready, 1)

                for f in range(0, FC, 2):
                    dve.wait_ge(inv_ready, 2 * l + f // 2 + 1)
                    error(f)
                    dve.wait_ge(num_done, 2 * l + f // 2 + 1)
                    a = product(f)
                    error(f + 1)
                    a = quotient(f, a)
                    b = product(f + 1)
                    total(f, a)
                    b = quotient(f + 1, b)
                    total(f + 1, b)
                for n in range(NT):
                    dve.wait_ge(row_done, NT * l + n + 1)
                    row_stats(ps_row[:, n, :], n)
                for n in range(NT):
                    row_scaled(l + 1, ps_row[:, n, :], n, z[:, n, :]).then_inc(z_ready, 1)

            layer(0, False)
            before = steps.n
            with dve.Fori(1, LAST) as l:
                steps.enter((l - 1) * LAYER_STEPS + before)
                layer(l, True)
                steps.leave()
            steps.enter(before + (LAST - 1) * LAYER_STEPS)
            layer(LAST, True)

            dve.wait_ge(fin_in, 32)
            dve.wait_ge(z_ready, NT * (L + 1))
            for n in range(NT):
                steps.then(nc.vector.tensor_tensor(z[:, n, :], z[:, n, :], fin_g[:], ALU.mult))
                steps.then(nc.vector.tensor_tensor(z[:, n, :], z[:, n, :], fin_b[:], ALU.add))
                steps.then(nc.vector.tensor_tensor(x0[:, n, :], x0[:, n, :], z[:, n, :], ALU.add))
                row_stats(x0[:, n, :], n)
            for n in range(NT):
                steps.then(row_scaled(L + 1, x0[:, n, :], n, z[:, n, :]))
                nc.vector.tensor_scalar(xs[:, n, :], z[:, n, :], 0.0, None, ALU.max).then_inc(xs_ready, 1)

            SAGE_STEPS = 10
            before = steps.base + steps.n
            sage_steps = Steps(dve, dve_steps, SAGE_STEPS)
            steps = sage_steps
            with dve.Fori(0, M) as m:
                steps.enter(m * SAGE_STEPS + before)
                for n in range(NT):
                    dve.wait_ge(xs_hi_ready, NT * m + n + 1)
                    nc.vector.tensor_tensor(ex_lo[:, n, :], xs[:, n, :], ex_hi[:, n, :].bitcast(F32),
                                            ALU.subtract).then_inc(xs_lo_ready, 1)
                dve.wait_ge(graph_ready, 2)
                for f in range(FC):
                    if f % 2 == 0:
                        dve.wait_ge(nsum_done, 2 * m + f // 2 + 1)
                    nc.vector.tensor_tensor(t[:, f, :], ps_num[:, f, :], inv_cnt[:], ALU.mult).then_inc(agg_ready, 1)
                for n in range(NT):
                    dve.wait_ge(srow_done, NT * m + n + 1)
                    row_stats(ps_row[:, n, :], n)
                dve.wait_ge(sgb_in, 32 * (m + 1))
                for n in range(NT):
                    steps.then(row_scaled(m + L + 2, ps_row[:, n, :], n, z[:, n, :]))
                    steps.then(nc.vector.tensor_tensor(z[:, n, :], z[:, n, :], s_g[:], ALU.mult))
                    steps.then(nc.vector.tensor_tensor(z[:, n, :], z[:, n, :], s_beta[:], ALU.add))
                    nc.vector.scalar_tensor_tensor(out=xs[:, n, :], in0=z[:, n, :], scalar=0.0, in1=xs[:, n, :],
                                                   op0=ALU.max, op1=ALU.add).then_inc(xs_ready, 1)
                steps.leave()
            dve.wait_ge(xs_ready, NT * (M + 1))
            nc.vector.tensor_tensor(h[:], x0[:], xs[:], ALU.add).then_inc(out_ready, 1)

        @block.tensor
        def _(pe):
            def count_edges(turn, first):
                for u in range(EU):
                    e = turn * EU + u
                    pe.wait_ge(hot_ready, e + 1)
                    for n in range(NT):
                        ins = nc.tensor.matmul(ps_adj[:, n, :], hot_src[:, e, n * P:(n + 1) * P],
                                               hot_dst[:, e, :], start=(first and u == 0 and n == 0),
                                               stop=True, skip_group_check=True)
                ins.then_inc(adj_done, 1)

            def transposed(i, rows, ready):
                for n in range(NT):
                    pe.wait_ge(ready, NT * i + n + 1)
                    for f in range(FC):
                        ins = nc.tensor.transpose(ps_zt[:, f, n * P:(n + 1) * P], rows[:, n, f * P:(f + 1) * P], ident[:])
                        if n == NT - 1 and f % 2 == 1:
                            ins.then_inc(zt_done if rows is z else xt_done, 1)

            def warm(to, count):
                for _ in range(count):
                    nc.tensor.matmul(to, hot_src[:, 0, 0:P], hot_src[:, 0:2, :], start=True, stop=True)

            def row_product(mat, column, done, to, start=True):
                for g in range(2):
                    for k in range(FC):
                        ins = nc.tensor.matmul(to[g], column[:, k:k + 1].broadcast_to([P, P]),
                                               mat[:, k, g * H // 2:(g + 1) * H // 2],
                                               start=(k == 0 and start), stop=True,
                                               skip_group_check=True)
                    ins.then_inc(done, 1)

            def virtual_node(l):
                pe.wait_ge(w1_in, 32 * l)
                for g in range(2):
                    nc.tensor.matmul(ps_v[g], ones[0:1, :], b1[:, g * H // 2:(g + 1) * H // 2], start=True, stop=True,
                                     skip_group_check=True)
                pe.wait_ge(vin_ready, l)
                row_product(w1, vsum, vn1_done, ps_v, False)

            def top_rows(l, last):
                pe.wait_ge(max_ready, 2 * (l + 1))
                for g in range(2):
                    for c in range(FC // 2):
                        f = g * FC // 2 + c
                        ins = nc.tensor.matmul(ps_top[g][:, c * P:(c + 1) * P], max_b2[:, f:f + 1].broadcast_to([P, P]),
                                               ident[:], start=(c == 0), stop=True, skip_group_check=True)
                    if last:
                        ins.then_inc(top_done, 1)
                if not isinstance(l, int):
                    pe.wait_ge(h_ready, NT * l)
                for f in range(FC):
                    pe.wait_ge(e_ready, FC * l + f + 1)
                    for n in range(NT):
                        ins = nc.tensor.transpose(ps_row[:, n, f * P:(f + 1) * P], e[:, f, n * P:(n + 1) * P], ident[:])
                ins.then_inc(et_done, NT)

            def summed(to, n, halves, first, done):
                for f in range(FC):
                    for g, half in enumerate(halves):
                        ins = nc.tensor.matmul(to[:, f, :], half[:, n, f * P:(f + 1) * P], adj[:, n, :],
                                               start=(first and f % 2 == 0 and g == 0), stop=True,
                                               skip_group_check=True)
                    if n == NT - 1 and f % 2 == 1:
                        ins.then_inc(done, 1)

            def layer(l, net):
                warm(ps_den[:, 0:2, :], WARM_NORM)
                transposed(l, z, z_ready)
                warm(ps_den[:, 0:2, :], WARM_RELU)
                if net:
                    virtual_node(l)
                top_rows(l, not net)
                if net:
                    warm(ps_den[:, 0:2, :], WARM_HIDDEN)
                    pe.wait_ge(w2_in, 16 * l)
                    pe.wait_ge(hid_ready, l)
                    row_product(w2, hid, top_done, ps_top, False)
                    warm(ps_den[:, 0:2, :], WARM_TOP)
                    pe.wait_ge(top_row_ready, 2 * l)
                    for f in range(FC):
                        ins = nc.tensor.matmul(ps_top_col[:, f:f + 1], top_row[:, f * P:(f + 1) * P], ones[0:1, 0:1],
                                               start=(f == 0), stop=True, skip_group_check=True)
                    ins.then_inc(top_col_done, 1)
                if not net:
                    pe.wait_ge(graph_ready, 1)
                warm(ps_den[:, 0:2, :], WARM_EXP)
                for f in range(FC):
                    nc.tensor.matmul(ps_den[:, f, :], ones_r[0:1, :], no_in[0:1, :], start=(f % 2 == 0), stop=True,
                                     skip_group_check=True)
                for n in range(NT):
                    pe.wait_ge(ex_lo_ready, NT * l + n + 1)
                    summed(ps_den, n, (ex_hi, ex_lo), False, den_done)
                for n in range(NT):
                    pe.wait_ge(dex_lo_ready, NT * l + n + 1)
                    summed(ps_num, n, (dex_hi, dex_lo), n == 0, num_done)
                if net:
                    pe.wait_ge(hb_ready, l)
                else:
                    pe.wait_ge(bias_in, 16)
                for n in range(NT):
                    nc.tensor.matmul(ps_row[:, n, :], ident[:], hb[:, n, :] if net else bias[:], start=True, stop=False)
                pe.wait_ge(w_in, 16 * (l + 1))
                for f in range(FC):
                    pe.wait_ge(t_ready, FC * l + f + 1)
                    for n in range(NT):
                        ins = nc.tensor.matmul(ps_row[:, n, :], t[:, f, n * P:(n + 1) * P], w[:, f, :],
                                               start=False, stop=(f == FC - 1))
                        if f == FC - 1:
                            ins.then_inc(row_done, 1)

            count_edges(0, True)
            with pe.Fori(1, ET // EU) as turn:
                count_edges(turn, False)
            pe.wait_ge(adj_ready, 1)
            pe.wait_ge(const_ready, 3)
            for n in range(NT):
                ins = nc.tensor.matmul(ps_cnt, ones_r[:], adj[:, n, :], start=(n == 0), stop=(n == NT - 1))
            ins.then_inc(cnt_done, 1)
            pe.wait_ge(ident_ready, 1)
            layer(0, False)
            with pe.Fori(1, L) as l:
                layer(l, True)

            with pe.Fori(0, M) as m:
                pe.wait_ge(srow_in, 16 * (m + 1))
                pe.wait_ge(h_ready, NT * L)
                transposed(m, xs, xs_ready)
                for n in range(NT):
                    nc.tensor.matmul(ps_row[:, n, :], ones[0:1, :], s_bias[:], start=True, stop=False)
                for n in range(NT):
                    pe.wait_ge(xs_lo_ready, NT * m + n + 1)
                    summed(ps_num, n, (ex_hi, ex_lo), n == 0, nsum_done)
                pe.wait_ge(wr_in, 16 * (m + 1))
                for f in range(FC):
                    if f % 2 == 0:
                        pe.wait_ge(xt_ready, 2 * m + f // 2 + 1)
                    for n in range(NT):
                        ins = nc.tensor.matmul(ps_row[:, n, :], h2[:, f, n * P:(n + 1) * P], wr[:, f, :],
                                               start=False, stop=False)
                ins.then_inc(xr_done, 1)
                pe.wait_ge(wl_in, 16 * (m + 1))
                pe.wait_ge(agg_ready, FC * (m + 1))
                for n in range(NT):
                    for f in range(FC):
                        ins = nc.tensor.matmul(ps_row[:, n, :], t[:, f, n * P:(n + 1) * P], wl[:, f, :],
                                               start=False, stop=(f == FC - 1))
                    ins.then_inc(srow_done, 1)


_OUT = ((256, 512), "float32")


def kernel(**inputs):
    import numpy as np
    import concourse.bacc as bacc
    from concourse.bass_utils import run_bass_kernel_spmd

    def columns(v):
        v = np.asarray(v)
        return v.reshape(v.shape[0], -1, P).transpose(0, 2, 1)

    g = {k: np.asarray(v) for k, v in inputs.items()}
    nets = g["L0_gnn_vn_W1"].shape[0]
    arrays = {
        "x": g["x"], "src": g["src"], "dst": g["dst"],
        "gcn_w": g["L0_gnn_gcn_W"], "gcn_b": g["L0_gnn_gcn_b"],
        "cols": np.stack([columns(g["L0_gnn_" + k][:nets]) for k in COLS], axis=2),
        "last_g": g["L0_gnn_norm_g"][nets], "last_b": g["L0_gnn_norm_b"][nets],
        "vn_emb": columns(g["L0_gnn_vn_emb"][None])[0],
        "vn_w1": g["L0_gnn_vn_W1"], "vn_b1": g["L0_gnn_vn_b1"], "vn_w2": g["L0_gnn_vn_W2"],
        "sage_wl": g["L1_gnn_W_l"].transpose(0, 2, 1), "sage_wr": g["L1_gnn_W_r"].transpose(0, 2, 1),
        "sage_b": g["L1_gnn_b"], "sage_g": g["L1_gnn_ln_g"], "sage_beta": g["L1_gnn_ln_b"],
    }
    arrays = {f"in_{k}": np.ascontiguousarray(v) for k, v in arrays.items()}
    nc = bacc.Bacc("TRN2", target_bir_lowering=False, num_devices=1)
    args = [nc.dram_tensor(k, v.shape, mybir.dt.from_np(v.dtype), kind="ExternalInput").ap() for k, v in arrays.items()]
    out = nc.dram_tensor("out_0", _OUT[0], mybir.dt.from_np(np.dtype(_OUT[1])), kind="ExternalOutput").ap()
    gnn_kernel(nc, *args, out)
    r = run_bass_kernel_spmd(nc, [arrays], core_ids=[0])
    return r.results[0]["out_0"]
```

```python
import concourse.bass as bass
from concourse import mybir
from contextlib import ExitStack

F32 = mybir.dt.float32
F32R = mybir.dt.float32r
BF16 = mybir.dt.bfloat16
I32 = mybir.dt.int32
ALU = mybir.AluOpType
ACT = mybir.ActivationFunctionType
AX_X = mybir.AxisListType.X

P = 128
LN_EPS = 1e-5
MSG_EPS = 1e-7
EXP_SHIFT = 32.0
WARM_NORM, WARM_RELU, WARM_HIDDEN, WARM_TOP, WARM_EXP, WARM_SUM = 8, 4, 4, 2, 1, 4
WARM_FINAL, WARM_SAGE, WARM_ROWS = 14, 5, 3
COLS = ("norm_g", "norm_b", "vn_g", "vn_beta", "vn_b2")


class Steps:

    def __init__(self, eng, sem, per_loop):
        self.eng, self.sem, self.per_loop = eng, sem, per_loop
        self.base, self.n = 0, 0

    def enter(self, base):
        self.base, self.n = base, 0

    def leave(self):
        assert self.n == self.per_loop, self.n

    def did(self, ins):
        ins.then_inc(self.sem, 1)
        self.n += 1
        return self.base + self.n

    def wait(self, value):
        self.eng.wait_ge(self.sem, value)

    def then(self, ins):
        self.wait(self.did(ins))


def gnn_kernel(nc, x, src, dst, gcn_w, gcn_b, cols, last_g, last_b, vn_emb, vn_w1, vn_b1, vn_w2,
               sage_wl, sage_wr, sage_b, sage_g, sage_beta, out):
    N, H = x.shape
    E = src.shape[0]
    L = gcn_w.shape[0]
    M = sage_wl.shape[0]
    NT = N // P
    FC = H // P
    ET = E // P
    EU = 8
    PARTS = [(n, slice(0, H)) for n in range(NT - 1)] + [(NT - 1, slice(0, H // 2)), (NT - 1, slice(H // 2, H))]
    Z_PARTS = len(PARTS)
    NCOL = len(COLS)
    LAST = L - 1

    ctx = ExitStack()
    with ctx:
        def sb(name, shape, dt=F32):
            return ctx.enter_context(nc.sbuf_tensor(name, shape, dt))

        def pb(name, shape):
            return ctx.enter_context(nc.psum_tensor(name, shape, F32))

        def sem(name):
            return ctx.enter_context(nc.semaphore(name))

        ident = sb("ident", [P, P])
        iota = sb("iota", [P, N], BF16)
        ones = sb("ones", [P, P])
        ones_r = sb("ones_r", [P, P], F32R)
        neg_half = sb("neg_half", [P, NT])
        shift = sb("shift", [P, 1])
        edge_i = sb("edge_i", [P, 2, ET], I32)
        edge_f = sb("edge_f", [P, 2, ET])
        hot_src = sb("hot_src", [P, ET, N], BF16)
        hot_dst = sb("hot_dst", [P, ET, N], BF16)
        adj = sb("adj", [P, NT, N], F32R)
        has_in = sb("has_in", [P, N])
        no_in = sb("no_in", [P, N], F32R)
        inv_cnt = sb("inv_cnt", [P, N])
        cnt1 = sb("cnt1", [P, N])
        x0 = sb("x0", [P, NT, H])
        h = sb("h", [P, NT, H])
        hb = sb("hb", [P, NT, H])
        z = sb("z", [P, NT, H])
        ex = sb("ex", [P, NT, H])
        dex = sb("dex", [P, NT, H])
        ex_hi = sb("ex_hi", [P, NT, H], F32R)
        ex_lo = sb("ex_lo", [P, NT, H], F32R)
        dex_hi = sb("dex_hi", [P, NT, H], F32R)
        dex_lo = sb("dex_lo", [P, NT, H], F32R)
        xs = sb("xs", [P, NT, H])
        d = sb("d", [P, NT, H])
        u_row = sb("u_row", [1, H])
        top_row = sb("top_row", [1, H])
        floor_row = sb("floor_row", [P, H])
        stats = sb("stats", [P, NT, 6])
        mv = sb("mv", [P, NT, 2])
        var_eps = sb("var_eps", [P, NT])
        rstd = sb("rstd", [P, NT])
        h2 = sb("h2", [P, FC, N])
        e = sb("e", [P, FC, N])
        gv = sb("gv", [P, FC, N])
        c = sb("c", [P, FC, N])
        r = sb("r", [P, FC, N])
        err = sb("err", [P, FC, N])
        pr = sb("pr", [P, FC, N])
        q = sb("q", [P, FC, N])
        lg = sb("lg", [P, FC, N])
        y = sb("y", [P, N])
        t = sb("t", [P, FC, N])
        t_hi = sb("t_hi", [P, FC, N], F32R)
        t_lo = sb("t_lo", [P, FC, N], F32R)
        h_sum = sb("h_sum", [P, FC])
        h_max = sb("h_max", [P, FC])
        neg_max = sb("neg_max", [P, FC])
        vn = sb("vn", [P, FC])
        vsum = sb("vsum", [P, FC])
        v_stats = sb("v_stats", [P, 2, 6])
        v_mv = sb("v_mv", [P, 2])
        vvar = sb("vvar", [P, 1])
        vrstd = sb("vrstd", [P, 1])
        ug = sb("ug", [P, FC])
        ub = sb("ub", [P, FC])
        hid = sb("hid", [P, FC])
        max_b2 = sb("max_b2", [P, FC])
        gm = sb("gm", [P, FC])
        w = sb("w", [P, FC, H])
        w_hi = sb("w_hi", [P, FC, H], F32R)
        w_lo = sb("w_lo", [P, FC, H], F32R)
        bias = sb("bias", [P, H])
        col = sb("col", [P, NCOL, FC])
        w1 = sb("w1", [P, FC, H])
        b1 = sb("b1", [1, H])
        w2 = sb("w2", [P, FC, H])
        wr, wl = w1, w2
        s_bias = sb("s_bias", [1, H])
        s_g = sb("s_g", [P, H])
        s_beta = sb("s_beta", [P, H])
        fin_g = sb("fin_g", [P, H])
        fin_b = sb("fin_b", [P, H])

        xt_hi = dex_hi[:].rearrange("p t (c n) -> p (t c) n", n=N)
        xt_lo = dex_lo[:].rearrange("p t (c n) -> p (t c) n", n=N)
        hot_pair = hot_dst[:].rearrange("p e n -> p (e n)").bitcast(F32R).rearrange("p (a c f) -> p a c f", a=2, c=FC)
        wr_hi, wr_lo = hot_pair[:, 0], hot_pair[:, 1]
        wl_hi, wl_lo = w_hi, w_lo

        ps_row = pb("ps_row", [P, NT, H])
        ps_zt = pb("ps_zt", [P, FC, N])
        ps_den = pb("ps_den", [P, FC, N])
        ps_num = pb("ps_num", [P, FC, N])
        ps_v = [ps_num[:, 0, :], ps_num[:, 2, :]]
        ps_top = [ps_zt[:, 0, :], ps_zt[:, 2, :]]
        ps_e = ps_den[:].rearrange("p (t c) n -> p t (c n)", t=NT)
        ps_u_col = ps_num[:, 1, 0:FC]
        ps_top_col = ps_zt[:, 1, 0:FC]
        ps_adj = ps_den[:, 0:2, :]
        ps_cnt = ps_den[:, 2, :]

        x_in, edge_in, emb_in, w_in, w1_in, w2_in = (sem(s) for s in ("x_in", "edge_in", "emb_in", "w_in", "w1_in", "w2_in"))
        bias_in, col_in, fin_in = sem("bias_in"), sem("col_in"), sem("fin_in")
        wr_in, wl_in, srow_in, sgb_in = sem("wr_in"), sem("wl_in"), sem("srow_in"), sem("sgb_in")
        out_done = sem("out_done")
        const_ready, iota_ready, ones_ready, ident_ready = sem("const_ready"), sem("iota_ready"), sem("ones_ready"), sem("ident_ready")
        hot_ready, adj_done, adj_ready, cnt_done, graph_ready = (sem(s) for s in (
            "hot_ready", "adj_done", "adj_ready", "cnt_done", "graph_ready"))
        var_ready, rstd_ready, z_ready, h_ready = sem("var_ready"), sem("rstd_ready"), sem("z_ready"), sem("h_ready")
        zt_done = sem("zt_done")
        h2_ready = sem("h2_ready")
        vin_ready, vn1_done, vvar_ready, vrstd_ready = (sem(s) for s in (
            "vin_ready", "vn1_done", "vvar_ready", "vrstd_ready"))
        hid_ready, top_done, vn_ready = sem("hid_ready"), sem("top_done"), sem("vn_ready")
        max_ready, e_ready, et_done, d_ready = sem("max_ready"), sem("e_ready"), sem("et_done"), sem("d_ready")
        v_stats_ready, u_row_ready, u_col_done = sem("v_stats_ready"), sem("u_row_ready"), sem("u_col_done")
        w_hi_ready, w_lo_ready, t_hi_ready = sem("w_hi_ready"), sem("w_lo_ready"), sem("t_hi_ready")
        t_lo_ready = sem("t_lo_ready")
        t_lo2_ready = sem("t_lo2_ready")
        gm_ready, gv_ready, c_ready, y_ready = sem("gm_ready"), sem("gv_ready"), sem("c_ready"), sem("y_ready")
        floor_ready, top_row_ready, top_col_done = (sem(s) for s in ("floor_ready", "top_row_ready", "top_col_done"))
        ex_ready, ex_hi_ready, ex_lo_ready, dex_ready, dex_hi_ready, dex_lo_ready = (sem(s) for s in (
            "ex_ready", "ex_hi_ready", "ex_lo_ready", "dex_ready", "dex_hi_ready", "dex_lo_ready"))
        den_done, num_done, t_ready, row_done, hb_ready = (sem(s) for s in (
            "den_done", "num_done", "t_ready", "row_done", "hb_ready"))
        sum_ready = sem("sum_ready")
        x0b_ready, rows_read, xt_hi_ready, xt_lo_ready = (sem(s) for s in (
            "x0b_ready", "rows_read", "xt_hi_ready", "xt_lo_ready"))
        wr_hi_ready, wr_lo_ready, wl_hi_ready, wl_lo_ready = (sem(s) for s in (
            "wr_hi_ready", "wr_lo_ready", "wl_hi_ready", "wl_lo_ready"))
        agg_hi_ready, agg_lo_ready = sem("agg_hi_ready"), sem("agg_lo_ready")
        xs_lo0_ready = sem("xs_lo0_ready")
        xs_ready, xs_hi_ready, xs_lo_ready, xt_done, xt_ready, nsum_done, agg_ready, xr_done, srow_done = (
            sem(s) for s in ("xs_ready", "xs_hi_ready", "xs_lo_ready", "xt_done", "xt_ready", "nsum_done",
                             "agg_ready", "xr_done", "srow_done"))
        log_ready, inv_ready = sem("log_ready"), sem("inv_ready")
        dve_steps, stats_seen = sem("dve_steps"), sem("stats_seen")
        out_ready = sem("out_ready")

        x_rows = x.rearrange("(t p) f -> p t f", p=P)
        out_rows = out.rearrange("(t p) f -> p t f", p=P)

        def spread(row):
            return row.partition_broadcast(P)

        def kchunks(mat):
            return mat.rearrange("(c p) f -> p c f", p=P)

        block = ctx.enter_context(nc.Block())

        @block.sync
        def _(sp):
            sp.dma_start(edge_i[:, 0, :], src.rearrange("(p j) -> p j", p=P)).then_inc(edge_in, 16)
            sp.dma_start(edge_i[:, 1, :], dst.rearrange("(p j) -> p j", p=P)).then_inc(edge_in, 16)
            sp.dma_start(x0[:], x_rows).then_inc(x_in, 16)
            sp.dma_start(vn[:], vn_emb).then_inc(emb_in, 16)
            sp.dma_start(w[:], kchunks(gcn_w[0])).then_inc(w_in, 16)
            sp.dma_start(bias[:], spread(gcn_b[0])).then_inc(bias_in, 16)
            sp.dma_start(col[:], cols[0]).then_inc(col_in, 16)
            sp.dma_start(w1[:], kchunks(vn_w1[0])).then_inc(w1_in, 16)
            sp.dma_start(b1[:], vn_b1[0:1, :]).then_inc(w1_in, 16)
            sp.dma_start(w2[:], kchunks(vn_w2[0])).then_inc(w2_in, 16)

            sp.dma_start(fin_g[:], spread(last_g)).then_inc(fin_in, 16)
            sp.dma_start(fin_b[:], spread(last_b)).then_inc(fin_in, 16)

            def layer_inputs(l, first):
                if not first:
                    sp.wait_ge(vn1_done, 2 * (l - 1))
                    sp.dma_start(w1[:], kchunks(vn_w1[l - 1])).then_inc(w1_in, 16)
                    sp.dma_start(b1[:], vn_b1[bass.ds(l - 1, 1), :]).then_inc(w1_in, 16)
                    sp.wait_ge(top_done, 2 * l)
                    sp.dma_start(w2[:], kchunks(vn_w2[l - 1])).then_inc(w2_in, 16)
                    sp.wait_ge(vn_ready, l - 1)
                    sp.dma_start(col[:], cols[l - 1]).then_inc(col_in, 16)
                    sp.wait_ge(hb_ready, l - 1)
                else:
                    sp.wait_ge(row_done, NT)
                sp.dma_start(bias[:], spread(gcn_b[l])).then_inc(bias_in, 16)
                sp.wait_ge(w_lo_ready, FC * l)
                sp.dma_start(w[:], kchunks(gcn_w[l])).then_inc(w_in, 16)

            layer_inputs(1, True)
            with sp.Fori(2, L) as l:
                layer_inputs(l, False)

            def sage_inputs(m):
                if isinstance(m, int):
                    sp.wait_ge(vn1_done, 2 * LAST)
                    sp.wait_ge(top_done, 2 * L)
                else:
                    sp.wait_ge(wr_lo_ready, FC * m)
                    sp.wait_ge(wl_lo_ready, FC * m)
                sp.dma_start(wr[:], kchunks(sage_wr[m])).then_inc(wr_in, 16)
                sp.dma_start(wl[:], kchunks(sage_wl[m])).then_inc(wl_in, 16)
                if not isinstance(m, int):
                    sp.wait_ge(xr_done, m)
                sp.dma_start(s_bias[:], sage_b[bass.ds(m, 1), :]).then_inc(srow_in, 16)
                if not isinstance(m, int):
                    sp.wait_ge(xs_ready, Z_PARTS * (m + 1))
                sp.dma_start(s_g[:], spread(sage_g[m])).then_inc(sgb_in, 16)
                sp.dma_start(s_beta[:], spread(sage_beta[m])).then_inc(sgb_in, 16)

            sage_inputs(0)
            with sp.Fori(1, M) as m:
                sage_inputs(m)
            for n in range(NT):
                sp.wait_ge(out_ready, (1, Z_PARTS)[n])
                sp.dma_start(out_rows[:, n, :], h[:, n, :]).then_inc(out_done, 16)
            sp.wait_ge(out_done, 16 * NT)

        @block.gpsimd
        def _(pool):
            nc.gpsimd.iota(iota[:], pattern=[[1, N]], base=0, channel_multiplier=0,
                           allow_small_or_imprecise_dtypes=True).then_inc(iota_ready, 1)
            nc.gpsimd.memset(neg_half[:], -0.5).then_inc(const_ready, 1)
            nc.gpsimd.memset(ident[:], 0.0).then_inc(const_ready, 1)
            pool.wait_ge(const_ready, 2)
            nc.gpsimd.affine_select(out=ident[:], in_=ident[:], compare_op=ALU.not_equal, fill=1.0, base=0,
                                    pattern=[[-1, P]], channel_multiplier=1).then_inc(ident_ready, 1)
            nc.gpsimd.memset(ones[:], 1.0).then_inc(ones_ready, 1)
            nc.gpsimd.memset(shift[:], EXP_SHIFT).then_inc(ones_ready, 1)

            def rstd_of(n):
                nc.gpsimd.tensor_tensor(rstd[:, n:n + 1], var_eps[:, n:n + 1], neg_half[:, n:n + 1],
                                        ALU.pow).then_inc(rstd_ready, 1)

            def row_rstd(i):
                for n in range(NT):
                    pool.wait_ge(var_ready, NT * i + n + 1)
                    rstd_of(n)

            def layer(l, net):
                if net:
                    pool.wait_ge(h_ready, NT * l)
                    pool.wait_ge(bias_in, 16 * (l + 1))
                    for n in range(NT):
                        ins = nc.gpsimd.tensor_tensor(hb[:, n, :], h[:, n, :], bias[:], ALU.add)
                    ins.then_inc(hb_ready, 1)
                    pool.wait_ge(vvar_ready, l)
                    nc.gpsimd.tensor_tensor(vrstd[:], vvar[:], neg_half[:, 0:1], ALU.pow).then_inc(vrstd_ready, 1)
                for f in range(FC):
                    pool.wait_ge(w_hi_ready, FC * l + f + 1)
                    nc.gpsimd.tensor_tensor(w_lo[:, f, :], w[:, f, :], w_hi[:, f, :].bitcast(F32),
                                            ALU.subtract).then_inc(w_lo_ready, 1)
                def gathered(f):
                    pool.wait_ge(gv_ready, FC * l + f + 1)
                    nc.gpsimd.tensor_tensor(c[:, f, :], h2[:, f, :], gv[:, f, :], ALU.add).then_inc(c_ready, 1)

                def total_lo(f):
                    pool.wait_ge(t_hi_ready, FC * l + f + 1)
                    nc.gpsimd.tensor_tensor(t_lo[:, f, :], t[:, f, :], t_hi[:, f, :].bitcast(F32),
                                            ALU.subtract).then_inc(t_lo_ready, 1)

                gathered(0)
                gathered(1)
                gathered(2)
                total_lo(0)
                gathered(3)
                total_lo(1)
                row_rstd(l + 1)

            row_rstd(0)
            layer(0, False)
            pool.wait_ge(fin_in, 32)
            for n in range(NT):
                nc.gpsimd.tensor_tensor(x0[:, n, :], x0[:, n, :], fin_b[:], ALU.add).then_inc(x0b_ready, 1)
            with pool.Fori(1, L) as l:
                layer(l, True)
            def low_halves(m, lo, hi, mat, hi_ready, lo_ready, feats):
                for f in feats:
                    pool.wait_ge(hi_ready, FC * m + f + 1)
                    nc.gpsimd.tensor_tensor(lo[:, f, :], mat[:, f, :], hi[:, f, :].bitcast(F32),
                                            ALU.subtract).then_inc(lo_ready, 1)

            def right(m, feats):
                low_halves(m, wr_lo, wr_hi, wr, wr_hi_ready, wr_lo_ready, feats)

            def next_round(m):
                pool.wait_ge(xs_hi_ready, Z_PARTS * m + 1)
                nc.gpsimd.tensor_tensor(ex_lo[:, 0, :], xs[:, 0, :], ex_hi[:, 0, :].bitcast(F32),
                                        ALU.subtract).then_inc(xs_lo0_ready, 1)
                right(m, range(FC - 1, FC))
                low_halves(m, wl_lo, wl_hi, wl, wl_hi_ready, wl_lo_ready, range(FC))

            right(0, range(FC - 1))
            row_rstd(L + 1)
            next_round(0)
            with pool.Fori(0, M - 1) as m:
                right(m + 1, range(2))
                pool.wait_ge(var_ready, NT * (m + L + 2) + 1)
                rstd_of(0)
                right(m + 1, range(2, FC - 1))
                pool.wait_ge(var_ready, NT * (m + L + 3))
                rstd_of(1)
                next_round(m + 1)
            pool.wait_ge(xs_ready, Z_PARTS * M)
            for n in range(NT):
                nc.gpsimd.tensor_tensor(x0[:, n, :], x0[:, n, :], xs[:, n, :], ALU.add).then_inc(sum_ready, 1)
            row_rstd(M + L + 1)

        @block.scalar
        def _(act):
            nc.scalar.preload_act_table_set("natural_log_exp_and_others")

            def keep_rows(l, n):
                act.wait_ge(z_ready, Z_PARTS * (l + 1) + (1, Z_PARTS)[n])
                nc.scalar.copy(h[:, n, :], ps_row[:, n, :]).then_inc(h_ready, 1)

            def layer(l, net):
                if net:
                    keep_rows(l - 1, 0)
                    act.wait_ge(col_in, 16 * l)
                    act.wait_ge(zt_done, 2 * l + 1)
                    for f in range(FC - 1):
                        if f == FC // 2:
                            act.wait_ge(y_ready, l)
                        nc.scalar.activation(h2[:, f, :], ps_zt[:, f, :], ACT.Relu, bias=col[:, 1, f:f + 1],
                                             scale=col[:, 0, f:f + 1],
                                             accum_out=h_sum[:, f:f + 1]).then_inc(h2_ready, 1)
                    keep_rows(l - 1, 1)
                else:
                    for f in range(0, FC, 2):
                        act.wait_ge(zt_done, f // 2 + 1)
                        nc.scalar.activation(h2[:, f:f + 2, :], ps_zt[:, f:f + 2, :], ACT.Relu).then_inc(h2_ready, 1)
                    act.wait_ge(ones_ready, 2)
                act.wait_ge(max_ready, 2 * l + 1)
                for f in range(FC):
                    nc.scalar.activation(e[:, f, :], h2[:, f, :], ACT.Identity,
                                         bias=neg_max[:, f:f + 1]).then_inc(e_ready, 1)
                if net:
                    for g in range(2):
                        act.wait_ge(v_stats_ready, 2 * l - 1 + g)
                        nc.scalar.copy(u_row[:, g * H // 2:(g + 1) * H // 2], ps_v[g][0:1, :]).then_inc(u_row_ready, 1)

                act.wait_ge(w_in, 16 * (l + 1))
                if net:
                    act.wait_ge(row_done, NT * l)
                for f in range(FC):
                    nc.scalar.copy(w_hi[:, f, :], w[:, f, :]).then_inc(w_hi_ready, 1)

                def weight(g):
                    half = slice(g * H // 2, (g + 1) * H // 2)
                    act.wait_ge(d_ready, 2 * l + g + 1)
                    nc.scalar.activation(ex[:, :, half], d[:, :, half], ACT.Exp, bias=shift[:]).then_inc(ex_ready, 1)
                    act.wait_ge(ex_ready, 2 * l + g + 1)
                    nc.scalar.copy(ex_hi[:, :, half], ex[:, :, half]).then_inc(ex_hi_ready, 1)

                def weighted_hi(g):
                    half = slice(g * H // 2, (g + 1) * H // 2)
                    act.wait_ge(dex_ready, 2 * l + g + 1)
                    nc.scalar.copy(dex_hi[:, :, half], dex[:, :, half]).then_inc(dex_hi_ready, 1)

                def top_row_half(g):
                    act.wait_ge(floor_ready, 2 * l + g + 1)
                    nc.scalar.copy(top_row[:, g * H // 2:(g + 1) * H // 2], ps_top[g][0:1, :]).then_inc(top_row_ready, 1)

                def log_den(g):
                    act.wait_ge(den_done, 2 * l + g + 1)
                    nc.scalar.activation(lg[:, 2 * g:2 * g + 2, :], ps_den[:, 2 * g:2 * g + 2, :],
                                         ACT.Ln).then_inc(log_ready, 1)

                def guess(g):
                    act.wait_ge(log_ready, 2 * l + g + 1)
                    nc.scalar.activation(r[:, 2 * g:2 * g + 2, :], lg[:, 2 * g:2 * g + 2, :], ACT.Exp,
                                         scale=-1.0).then_inc(inv_ready, 1)

                def added(f):
                    nc.scalar.activation(gv[:, f, :], has_in[:], ACT.Identity, bias=vn[:, f:f + 1],
                                         scale=gm[:, f:f + 1]).then_inc(gv_ready, 1)

                def total_hi(f):
                    act.wait_ge(t_ready, FC * l + f + 1)
                    nc.scalar.copy(t_hi[:, f, :], t[:, f, :]).then_inc(t_hi_ready, 1)

                if net:
                    top_row_half(0)
                weight(0)
                if net:
                    top_row_half(1)
                weight(1)
                weighted_hi(0)
                log_den(0)
                guess(0)
                weighted_hi(1)
                act.wait_ge(gm_ready, l + 1)
                if net:
                    act.wait_ge(vn_ready, l)
                added(0)
                added(1)
                log_den(1)
                guess(1)
                total_hi(0)
                added(2)
                total_hi(1)
                added(3)
                total_hi(2)
                total_hi(3)
            layer(0, False)
            with act.Fori(1, L) as l:
                layer(l, True)

            def high_halves(m, hi, mat, landed, ready):
                act.wait_ge(landed, 16 * (m + 1))
                for f in range(FC):
                    nc.scalar.copy(hi[:, f, :], mat[:, f, :]).then_inc(ready, 1)

            def rows_hi(m):
                for k, (n, part) in enumerate(PARTS):
                    act.wait_ge(xs_ready, Z_PARTS * m + k + 1)
                    nc.scalar.copy(ex_hi[:, n, part], xs[:, n, part]).then_inc(xs_hi_ready, 1)

            def sage(m, last):
                for g in range(2):
                    act.wait_ge(xt_done, 2 * m + g + 1)
                    nc.scalar.copy(xt_hi[:, 2 * g:2 * g + 2, :], ps_zt[:, 2 * g:2 * g + 2, :]).then_inc(xt_hi_ready, 1)
                for f in range(FC):
                    act.wait_ge(agg_ready, FC * m + f + 1)
                    nc.scalar.copy(t_hi[:, f, :], t[:, f, :]).then_inc(agg_hi_ready, 1)
                if not last:
                    act.wait_ge(xr_done, m + 1)
                    high_halves(m + 1, wr_hi, wr, wr_in, wr_hi_ready)
                    act.wait_ge(srow_done, NT * (m + 1))
                    high_halves(m + 1, wl_hi, wl, wl_in, wl_hi_ready)
                    rows_hi(m + 1)

            high_halves(0, wr_hi, wr, wr_in, wr_hi_ready)
            act.wait_ge(row_done, NT * L)
            high_halves(0, wl_hi, wl, wl_in, wl_hi_ready)
            rows_hi(0)
            with act.Fori(0, M - 1) as m:
                sage(m, False)
            sage(M - 1, True)

        @block.vector
        def _(dve):
            LAYER_STEPS = 19
            steps = Steps(dve, dve_steps, LAYER_STEPS)

            dve.wait_ge(ones_ready, 1)
            nc.vector.tensor_copy(ones_r[:], ones[:]).then_inc(const_ready, 1)
            dve.wait_ge(edge_in, 32)
            steps.then(nc.vector.tensor_copy(edge_f[:], edge_i[:]))
            dve.wait_ge(iota_ready, 1)
            with dve.Fori(0, ET // EU) as turn:
                for e in range(EU):
                    e = turn * EU + e
                    nc.vector.tensor_scalar(hot_src[:, e, :], iota[:], edge_f[:, 0, bass.ds(e, 1)], None,
                                            ALU.is_equal)
                    ins = nc.vector.tensor_scalar(hot_dst[:, e, :], iota[:], edge_f[:, 1, bass.ds(e, 1)], None,
                                                  ALU.is_equal)
                    ins.then_inc(hot_ready, 1)

            def row_stats(rows, n):
                got = steps.did(nc.vector.bn_stats(stats[:, n, :], rows))
                steps.wait(got)
                dve.sem_inc(stats_seen, 1)
                steps.then(nc.vector.bn_aggr(mv[:, n, :], stats[:, n, :]))
                nc.vector.tensor_scalar(var_eps[:, n:n + 1], mv[:, n, 1:2], LN_EPS, None, ALU.add).then_inc(var_ready, 1)

            def row_scaled(i, rows, n, to):
                dve.wait_ge(rstd_ready, NT * i + n + 1)
                return nc.vector.tensor_scalar(to, rows, mv[:, n, 0:1], rstd[:, n:n + 1], ALU.subtract, ALU.mult)

            def z_rows(i, rows):
                for n, part in PARTS:
                    row_scaled(i, rows[:, n, part], n, z[:, n, part]).then_inc(z_ready, 1)

            dve.wait_ge(x_in, 16)
            for n in range(NT):
                row_stats(x0[:, n, :], n)
            z_rows(0, x0)

            dve.wait_ge(adj_done, ET // EU)
            nc.vector.tensor_copy(adj[:], ps_adj).then_inc(adj_ready, 1)
            dve.wait_ge(cnt_done, 1)
            a = steps.did(nc.vector.tensor_scalar(has_in[:], ps_cnt, 1.0, None, ALU.min))
            b = steps.did(nc.vector.tensor_scalar(cnt1[:], ps_cnt, 1.0, None, ALU.max))
            steps.wait(a)
            nc.vector.tensor_scalar(no_in[:], has_in[:], -1.0, 1.0, ALU.mult, ALU.add).then_inc(graph_ready, 1)

            def largest(offset):
                steps.then(nc.vector.tensor_reduce(h_max[:], h2[:], AX_X, ALU.max))
                nc.vector.tensor_scalar(neg_max[:], h_max[:], -1.0, None, ALU.mult).then_inc(max_ready, 1)
                nc.vector.tensor_tensor(max_b2[:], h_max[:], offset, ALU.add).then_inc(max_ready, 1)

            def virtual_node(l):
                nc.vector.tensor_tensor(vsum[:], h_sum[:], vn[:], ALU.add).then_inc(vin_ready, 1)
                largest(col[:, 4, :])
                for g in range(2):
                    dve.wait_ge(vn1_done, 2 * l - 1 + g)
                    nc.vector.bn_stats(v_stats[:, g, :], ps_v[g]).then_inc(v_stats_ready, 1)
                dve.wait_ge(v_stats_ready, 2 * l)
                dve.sem_inc(stats_seen, 1)
                steps.then(nc.vector.bn_aggr(v_mv[:], v_stats[:]))
                nc.vector.tensor_scalar(vvar[:], v_mv[:, 1:2], LN_EPS, None, ALU.add).then_inc(vvar_ready, 1)
                dve.wait_ge(u_col_done, l)
                steps.then(nc.vector.scalar_tensor_tensor(out=ug[:], in0=ps_u_col, scalar=v_mv[:, 0:1], in1=col[:, 2, :],
                                                          op0=ALU.subtract, op1=ALU.mult))
                dve.wait_ge(vrstd_ready, l)
                steps.then(nc.vector.scalar_tensor_tensor(out=ub[:], in0=ug[:], scalar=vrstd[:], in1=col[:, 3, :],
                                                          op0=ALU.mult, op1=ALU.add))
                nc.vector.tensor_scalar(hid[:], ub[:], 0.0, None, ALU.max).then_inc(hid_ready, 1)

            def layer(l, net):
                if net:
                    dve.wait_ge(col_in, 16 * l)
                    dve.wait_ge(zt_done, 2 * l + 2)
                    f = FC - 1
                    nc.vector.tensor_scalar(y[:], ps_zt[:, f, :], col[:, 0, f:f + 1], col[:, 1, f:f + 1],
                                            ALU.mult, ALU.add).then_inc(y_ready, 1)
                    dve.wait_ge(y_ready, l)
                    steps.then(nc.vector.tensor_scalar(h2[:, f, :], y[:], 0.0, 0.0, ALU.max, ALU.add,
                                                       accum_out=h_sum[:, f:f + 1]))
                dve.wait_ge(h2_ready, (FC - 1) * l + 2)
                if net:
                    virtual_node(l)
                else:
                    dve.wait_ge(emb_in, 16)
                    largest(vn[:])
                for g in range(2):
                    half = slice(g * H // 2, (g + 1) * H // 2)
                    dve.wait_ge(top_done, 2 * l + g + 1)
                    nc.vector.tensor_scalar(floor_row[:, half], ps_top[g], -1.0, 0.0,
                                            ALU.mult, ALU.min).then_inc(floor_ready, 1)
                    dve.wait_ge(floor_ready, 2 * l + g + 1)
                    if g == 0:
                        dve.wait_ge(et_done, l + 1)
                    nc.vector.tensor_tensor(d[:, :, half], ps_e[:, :, half],
                                            floor_row[:, None, half].broadcast_to([P, NT, H // 2]),
                                            ALU.max).then_inc(d_ready, 1)

                def low(g):
                    half = slice(g * H // 2, (g + 1) * H // 2)
                    dve.wait_ge(ex_hi_ready, 2 * l + g + 1)
                    nc.vector.tensor_tensor(ex_lo[:, :, half], ex[:, :, half], ex_hi[:, :, half].bitcast(F32),
                                            ALU.subtract).then_inc(ex_lo_ready, 1)

                def weighted(g):
                    half = slice(g * H // 2, (g + 1) * H // 2)
                    dve.wait_ge(ex_ready, 2 * l + g + 1)
                    nc.vector.tensor_tensor(dex[:, :, half], d[:, :, half], ex[:, :, half],
                                            ALU.mult).then_inc(dex_ready, 1)

                def weighted_low(g):
                    half = slice(g * H // 2, (g + 1) * H // 2)
                    dve.wait_ge(dex_hi_ready, 2 * l + g + 1)
                    nc.vector.tensor_tensor(dex_lo[:, :, half], dex[:, :, half], dex_hi[:, :, half].bitcast(F32),
                                            ALU.subtract).then_inc(dex_lo_ready, 1)

                def error(g):
                    dve.wait_ge(inv_ready, 2 * l + g + 1)
                    steps.did(nc.vector.tensor_tensor(err[:, 2 * g:2 * g + 2, :], ps_den[:, 2 * g:2 * g + 2, :],
                                                      r[:, 2 * g:2 * g + 2, :], ALU.mult))

                def totals(g):
                    pair = range(2 * g, 2 * g + 2)
                    dve.wait_ge(num_done, 2 * l + g + 1)
                    got = [steps.did(nc.vector.tensor_tensor(pr[:, f, :], ps_num[:, f, :], r[:, f, :], ALU.mult))
                           for f in pair]
                    for k, f in enumerate(pair):
                        steps.wait(got[k])
                        got[k] = steps.did(nc.vector.scalar_tensor_tensor(
                            out=q[:, f, :], in0=err[:, f, :], scalar=-2.0, in1=pr[:, f, :], op0=ALU.add, op1=ALU.mult))
                    for k, f in enumerate(pair):
                        steps.wait(got[k])
                        if k == 0:
                            dve.wait_ge(c_ready, FC * l + f + 2)
                        nc.vector.tensor_tensor(t[:, f, :], c[:, f, :], q[:, f, :], ALU.subtract).then_inc(t_ready, 1)

                low(0)
                weighted(0)
                low(1)
                weighted_low(0)
                if net:
                    dve.wait_ge(top_col_done, l)
                nc.vector.tensor_scalar(gm[:], ps_top_col if net else max_b2[:], 0.0, MSG_EPS,
                                        ALU.max, ALU.add).then_inc(gm_ready, 1)
                if net:
                    nc.vector.tensor_tensor(vn[:], ps_top_col, h_max[:], ALU.subtract).then_inc(vn_ready, 1)
                weighted(1)
                error(0)
                weighted_low(1)
                totals(0)
                error(1)
                totals(1)
                for f in range(FC // 2, FC):
                    dve.wait_ge(t_hi_ready, FC * l + f + 1)
                    nc.vector.tensor_tensor(t_lo[:, f, :], t[:, f, :], t_hi[:, f, :].bitcast(F32),
                                            ALU.subtract).then_inc(t_lo2_ready, 1)
                for n in range(NT):
                    dve.wait_ge(row_done, NT * l + n + 1)
                    row_stats(ps_row[:, n, :], n)
                if not (isinstance(l, int) and l == LAST):
                    z_rows(l + 1, ps_row)

            layer(0, False)
            before = steps.n
            with dve.Fori(1, LAST) as l:
                steps.enter((l - 1) * LAYER_STEPS + before)
                layer(l, True)
                steps.leave()
            steps.enter(before + (LAST - 1) * LAYER_STEPS)
            layer(LAST, True)

            steps.wait(b)
            steps.then(nc.vector.reciprocal(inv_cnt[:], cnt1[:]))

            def gained(n, gain):
                nc.vector.scalar_tensor_tensor(out=z[:, n, :], in0=ps_row[:, n, :], scalar=mv[:, n, 0:1], in1=gain[:],
                                               op0=ALU.subtract, op1=ALU.mult).then_inc(rows_read, 1)

            dve.wait_ge(fin_in, 32)
            dve.wait_ge(x0b_ready, NT)
            for n in range(NT):
                gained(n, fin_g)
            for n in range(NT):
                dve.wait_ge(rows_read, n + 1)
                dve.wait_ge(rstd_ready, NT * L + n + 1)
                steps.then(nc.vector.scalar_tensor_tensor(out=x0[:, n, :], in0=z[:, n, :], scalar=rstd[:, n:n + 1],
                                                          in1=x0[:, n, :], op0=ALU.mult, op1=ALU.add))
                row_stats(x0[:, n, :], n)
            for n in range(NT):
                above = steps.did(nc.vector.tensor_scalar(z[:, n, :], x0[:, n, :], mv[:, n, 0:1], 0.0,
                                                          ALU.subtract, ALU.max))
            steps.wait(above)
            for n, part in PARTS:
                dve.wait_ge(rstd_ready, NT * (L + 1) + n + 1)
                nc.vector.tensor_scalar(xs[:, n, part], z[:, n, part], rstd[:, n:n + 1], None,
                                        ALU.mult).then_inc(xs_ready, 1)

            SAGE_STEPS = 7
            before = steps.base + steps.n
            steps = Steps(dve, dve_steps, SAGE_STEPS)

            def sage(m, last):
                for k in range(1, Z_PARTS):
                    n, part = PARTS[k]
                    dve.wait_ge(xs_hi_ready, Z_PARTS * m + k + 1)
                    nc.vector.tensor_tensor(ex_lo[:, n, part], xs[:, n, part], ex_hi[:, n, part].bitcast(F32),
                                            ALU.subtract).then_inc(xs_lo_ready, 1)
                for f in range(FC):
                    if f % 2 == 0:
                        dve.wait_ge(nsum_done, 2 * m + f // 2 + 1)
                    nc.vector.tensor_tensor(t[:, f, :], ps_num[:, f, :], inv_cnt[:], ALU.mult).then_inc(agg_ready, 1)
                for g in range(2):
                    dve.wait_ge(xt_hi_ready, 2 * m + g + 1)
                    nc.vector.tensor_tensor(xt_lo[:, 2 * g:2 * g + 2, :], ps_zt[:, 2 * g:2 * g + 2, :],
                                            xt_hi[:, 2 * g:2 * g + 2, :].bitcast(F32),
                                            ALU.subtract).then_inc(xt_lo_ready, 1)
                for f in range(FC):
                    dve.wait_ge(agg_hi_ready, FC * m + f + 1)
                    nc.vector.tensor_tensor(t_lo[:, f, :], t[:, f, :], t_hi[:, f, :].bitcast(F32),
                                            ALU.subtract).then_inc(agg_lo_ready, 1)
                dve.wait_ge(sgb_in, 32 * (m + 1))

                def offset(n, part):
                    dve.wait_ge(rstd_ready, NT * (m + L + 2) + n + 1)
                    return steps.did(nc.vector.scalar_tensor_tensor(
                        out=z[:, n, part], in0=z[:, n, part], scalar=rstd[:, n:n + 1], in1=s_beta[:, part],
                        op0=ALU.mult, op1=ALU.add))

                def added(n, part):
                    nc.vector.scalar_tensor_tensor(
                        out=(h if last else xs)[:, n, part], in0=z[:, n, part], scalar=0.0,
                        in1=(x0 if last else xs)[:, n, part], op0=ALU.max,
                        op1=ALU.add).then_inc(out_ready if last else xs_ready, 1)

                if last:
                    dve.wait_ge(sum_ready, NT)
                for n in range(NT):
                    dve.wait_ge(srow_done, NT * m + n + 1)
                    row_stats(ps_row[:, n, :], n)
                    gained(n, s_g)
                    dve.wait_ge(rows_read, NT * (m + 1) + n + 1)
                    parts = [part for tile, part in PARTS if tile == n]
                    for part in parts:
                        done = offset(n, part)
                    steps.wait(done)
                    for part in parts:
                        added(n, part)

            with dve.Fori(0, M - 1) as m:
                steps.enter(m * SAGE_STEPS + before)
                sage(m, False)
                steps.leave()
            steps.enter((M - 1) * SAGE_STEPS + before)
            sage(M - 1, True)

        @block.tensor
        def _(pe):
            def count_edges(turn, first):
                for u in range(EU):
                    e = turn * EU + u
                    pe.wait_ge(hot_ready, e + 1)
                    for n in range(NT):
                        ins = nc.tensor.matmul(ps_adj[:, n, :], hot_src[:, e, n * P:(n + 1) * P],
                                               hot_dst[:, e, :], start=(first and u == 0 and n == 0),
                                               stop=True, skip_group_check=True)
                ins.then_inc(adj_done, 1)

            def transposed(rows, arrived, done):
                for n in range(NT):
                    for f in range(FC):
                        arrived(n, f)
                        ins = nc.tensor.transpose(ps_zt[:, f, n * P:(n + 1) * P], rows[:, n, f * P:(f + 1) * P], ident[:])
                        if n == NT - 1 and f % 2 == 1:
                            ins.then_inc(done, 1)

            def warm(to, count):
                for _ in range(count):
                    nc.tensor.matmul(to, hot_src[:, 0, 0:P], hot_src[:, 0:2, :], start=True, stop=True)

            def row_product(mat, column, done, to, start=True):
                for g in range(2):
                    for k in range(FC):
                        ins = nc.tensor.matmul(to[g], column[:, k:k + 1].broadcast_to([P, P]),
                                               mat[:, k, g * H // 2:(g + 1) * H // 2],
                                               start=(k == 0 and start), stop=True,
                                               skip_group_check=True)
                    ins.then_inc(done, 1)

            def columns(to, row, feats, ready, value, done):
                pe.wait_ge(ready, value)
                nc.tensor.matmul(to[:, 0:1], hot_src[:, 0, 0:P], hot_src[:, 0, 0:1], start=True, stop=True)
                for f in feats:
                    ins = nc.tensor.transpose(to[:, f:f + 1], row[:, f * P:(f + 1) * P], ident[0:1, 0:1])
                ins.then_inc(done, 1)

            def virtual_node(l):
                pe.wait_ge(w1_in, 32 * l)
                for g in range(2):
                    nc.tensor.matmul(ps_v[g], ones[0:1, :], b1[:, g * H // 2:(g + 1) * H // 2], start=True, stop=True,
                                     skip_group_check=True)
                pe.wait_ge(vin_ready, l)
                row_product(w1, vsum, vn1_done, ps_v, False)

            def top_rows(l, last):
                pe.wait_ge(max_ready, 2 * (l + 1))
                for g in range(2):
                    for c in range(FC // 2):
                        f = g * FC // 2 + c
                        ins = nc.tensor.matmul(ps_top[g][:, c * P:(c + 1) * P], max_b2[:, f:f + 1].broadcast_to([P, P]),
                                               ident[:], start=(c == 0), stop=True, skip_group_check=True)
                    if last:
                        ins.then_inc(top_done, 1)
                if not last:
                    columns(ps_u_col, u_row, range(FC), u_row_ready, 2 * l, u_col_done)
                    pe.wait_ge(h_ready, NT * l)
                for f in range(FC):
                    pe.wait_ge(e_ready, FC * l + f + 1)
                    for n in range(NT):
                        ins = nc.tensor.transpose(ps_e[:, n, f * P:(f + 1) * P], e[:, f, n * P:(n + 1) * P], ident[:])
                ins.then_inc(et_done, 1)

            def summed(to, tiles, feats, halves, first, done):
                for n in tiles:
                    for f in feats:
                        for k, half in enumerate(halves):
                            ins = nc.tensor.matmul(to[:, f, :], half[:, n, f * P:(f + 1) * P], adj[:, n, :],
                                                   start=(first and n == tiles[0] and f % 2 == 0 and k == 0),
                                                   stop=True, skip_group_check=True)
                        if n == NT - 1 and f % 2 == 1:
                            ins.then_inc(done, 1)

            def layer(l, net):
                warm(ps_den[:, 0:2, :], WARM_NORM)

                def z_arrived(n, f):
                    if f == 0:
                        pe.wait_ge(z_ready, Z_PARTS * l + n + 1)
                    elif n == NT - 1 and f == FC // 2:
                        pe.wait_ge(z_ready, Z_PARTS * (l + 1))

                transposed(z, z_arrived, zt_done)
                warm(ps_den[:, 0:2, :], WARM_RELU)
                def base_rows():
                    if net:
                        pe.wait_ge(hb_ready, l)
                    else:
                        pe.wait_ge(bias_in, 16)
                    for n in range(NT):
                        nc.tensor.matmul(ps_row[:, n, :], ident[:], hb[:, n, :] if net else bias[:], start=True, stop=False)

                if net:
                    virtual_node(l)
                top_rows(l, not net)
                if net:
                    warm(ps_row[:, 0, :], WARM_HIDDEN)
                    pe.wait_ge(w2_in, 16 * l)
                    pe.wait_ge(hid_ready, l)
                    row_product(w2, hid, top_done, ps_top, False)
                    base_rows()
                    warm(ps_num[:, 2:4, :], WARM_TOP)
                if not net:
                    pe.wait_ge(graph_ready, 1)
                def den(g):
                    for f in feats[g]:
                        nc.tensor.matmul(ps_den[:, f, :], ones_r[0:1, :], no_in[0:1, :], start=(f % 2 == 0), stop=True,
                                         skip_group_check=True)
                    summed(ps_den, tiles, feats[g], (ex_hi, ex_lo), False, den_done)

                tiles, feats = range(NT), (range(FC // 2), range(FC // 2, FC))
                pe.wait_ge(ex_lo_ready, 2 * l + 1)
                den(0)
                if net:
                    columns(ps_top_col, top_row, range(FC), top_row_ready, 2 * l, top_col_done)
                warm(ps_num[:, 2:4, :], WARM_EXP)
                pe.wait_ge(dex_lo_ready, 2 * l + 1)
                summed(ps_num, tiles, feats[0], (dex_hi, dex_lo), True, num_done)
                pe.wait_ge(ex_lo_ready, 2 * l + 2)
                den(1)
                pe.wait_ge(dex_lo_ready, 2 * l + 2)
                summed(ps_num, tiles, feats[1], (dex_hi, dex_lo), True, num_done)
                warm(ps_zt[:, 2:4, :], WARM_SUM)

                def linear_hi(n, f):
                    pe.wait_ge(t_hi_ready, FC * l + f + 1)
                    for half in (w_hi, w_lo):
                        nc.tensor.matmul(ps_row[:, n, :], t_hi[:, f, n * P:(n + 1) * P], half[:, f, :],
                                         start=False, stop=False)

                def linear_lo(n, f):
                    if f in feats[0]:
                        pe.wait_ge(t_lo_ready, FC // 2 * l + f + 1)
                    else:
                        pe.wait_ge(t_lo2_ready, FC // 2 * (l - 1) + f + 1)
                    ins = nc.tensor.matmul(ps_row[:, n, :], t_lo[:, f, n * P:(n + 1) * P], w_hi[:, f, :],
                                           start=False, stop=(f == FC - 1))
                    if f == FC - 1:
                        ins.then_inc(row_done, 1)

                pe.wait_ge(w_lo_ready, FC * (l + 1))
                if not net:
                    base_rows()
                for linear in (linear_hi, linear_lo):
                    for f in feats[0]:
                        for n in range(NT):
                            linear(n, f)
                for n in range(NT):
                    for linear in (linear_hi, linear_lo):
                        for f in feats[1]:
                            linear(n, f)

            count_edges(0, True)
            with pe.Fori(1, ET // EU) as turn:
                count_edges(turn, False)
            pe.wait_ge(adj_ready, 1)
            pe.wait_ge(const_ready, 3)
            for n in range(NT):
                ins = nc.tensor.matmul(ps_cnt, ones_r[:], adj[:, n, :], start=(n == 0), stop=(n == NT - 1))
            ins.then_inc(cnt_done, 1)
            pe.wait_ge(ident_ready, 1)
            layer(0, False)
            with pe.Fori(1, L) as l:
                layer(l, True)

            def sage(m):
                warm(ps_den[:, 0:2, :], WARM_SAGE)
                pe.wait_ge(srow_in, 16 * (m + 1))
                for n in range(NT):
                    pe.wait_ge(rows_read, NT * m + n + 1)
                    nc.tensor.matmul(ps_row[:, n, :], ones[0:1, :], s_bias[:], start=True, stop=False)
                for k, (n, part) in enumerate(PARTS):
                    feats = range(part.start // P, part.stop // P)
                    pe.wait_ge(xs_ready, Z_PARTS * m + k + 1)
                    for f in feats:
                        ins = nc.tensor.transpose(ps_zt[:, f, n * P:(n + 1) * P], xs[:, n, f * P:(f + 1) * P], ident[:])
                    if n == NT - 1:
                        ins.then_inc(xt_done, 1)
                    if k == 0:
                        pe.wait_ge(xs_lo0_ready, m + 1)
                        summed(ps_num, (n,), feats, (ex_hi, ex_lo), True, nsum_done)
                        warm(ps_den[:, 0:2, :], WARM_ROWS)
                for k in range(1, Z_PARTS):
                    n, part = PARTS[k]
                    pe.wait_ge(xs_lo_ready, (Z_PARTS - 1) * m + k)
                    summed(ps_num, (n,), range(part.start // P, part.stop // P), (ex_hi, ex_lo), False, nsum_done)
                pe.wait_ge(wr_lo_ready, FC * (m + 1))
                for f in range(FC):
                    pe.wait_ge(xt_hi_ready, 2 * m + f // 2 + 1)
                    for n in range(NT):
                        for half in (wr_hi, wr_lo):
                            nc.tensor.matmul(ps_row[:, n, :], xt_hi[:, f, n * P:(n + 1) * P], half[:, f, :],
                                             start=False, stop=False)
                for f in range(FC):
                    pe.wait_ge(xt_lo_ready, 2 * m + f // 2 + 1)
                    for n in range(NT):
                        ins = nc.tensor.matmul(ps_row[:, n, :], xt_lo[:, f, n * P:(n + 1) * P], wr_hi[:, f, :],
                                               start=False, stop=False)
                ins.then_inc(xr_done, 1)
                pe.wait_ge(wl_lo_ready, FC * (m + 1))
                for n in range(NT):
                    for f in range(FC):
                        pe.wait_ge(agg_hi_ready, FC * m + f + 1)
                        for half in (wl_hi, wl_lo):
                            nc.tensor.matmul(ps_row[:, n, :], t_hi[:, f, n * P:(n + 1) * P], half[:, f, :],
                                             start=False, stop=False)
                    for f in range(FC):
                        pe.wait_ge(agg_lo_ready, FC * m + f + 1)
                        ins = nc.tensor.matmul(ps_row[:, n, :], t_lo[:, f, n * P:(n + 1) * P], wl_hi[:, f, :],
                                               start=False, stop=(f == FC - 1))
                    ins.then_inc(srow_done, 1)

            warm(ps_den[:, 0:2, :], WARM_FINAL)
            with pe.Fori(0, M) as m:
                sage(m)


_OUT = ((256, 512), "float32")


def kernel(**inputs):
    import numpy as np
    import concourse.bacc as bacc
    from concourse.bass_utils import run_bass_kernel_spmd

    def columns(v):
        v = np.asarray(v)
        return v.reshape(v.shape[0], -1, P).transpose(0, 2, 1)

    g = {k: np.asarray(v) for k, v in inputs.items()}
    nets = g["L0_gnn_vn_W1"].shape[0]
    arrays = {
        "x": g["x"], "src": g["src"], "dst": g["dst"],
        "gcn_w": g["L0_gnn_gcn_W"], "gcn_b": g["L0_gnn_gcn_b"],
        "cols": np.stack([columns(g["L0_gnn_" + k][:nets]) for k in COLS], axis=2),
        "last_g": g["L0_gnn_norm_g"][nets], "last_b": g["L0_gnn_norm_b"][nets],
        "vn_emb": columns(g["L0_gnn_vn_emb"][None])[0],
        "vn_w1": g["L0_gnn_vn_W1"], "vn_b1": g["L0_gnn_vn_b1"], "vn_w2": g["L0_gnn_vn_W2"],
        "sage_wl": g["L1_gnn_W_l"].transpose(0, 2, 1), "sage_wr": g["L1_gnn_W_r"].transpose(0, 2, 1),
        "sage_b": g["L1_gnn_b"], "sage_g": g["L1_gnn_ln_g"], "sage_beta": g["L1_gnn_ln_b"],
    }
    arrays = {f"in_{k}": np.ascontiguousarray(v) for k, v in arrays.items()}
    nc = bacc.Bacc("TRN2", target_bir_lowering=False, num_devices=1)
    args = [nc.dram_tensor(k, v.shape, mybir.dt.from_np(v.dtype), kind="ExternalInput").ap() for k, v in arrays.items()]
    out = nc.dram_tensor("out_0", _OUT[0], mybir.dt.from_np(np.dtype(_OUT[1])), kind="ExternalOutput").ap()
    gnn_kernel(nc, *args, out)
    r = run_bass_kernel_spmd(nc, [arrays], core_ids=[0])
    return r.results[0]["out_0"]
```
